# Optimizing a Trainium2 kernel written in Bass

```python
import numpy as np
import jax
import jax.numpy as jnp

def _softmax(x, axis=-1):
    return jax.nn.softmax(x, axis=axis)

def _gelu(x):
    return jax.nn.gelu(x, approximate=True)

def _silu(x):
    return jax.nn.silu(x)

def _sigmoid(x):
    return jax.nn.sigmoid(x)

def _layernorm(x, axis=-1, eps=1e-05):
    m = jnp.mean(x, axis=axis, keepdims=True)
    v = jnp.var(x, axis=axis, keepdims=True)
    return (x - m) / jnp.sqrt(v + eps)

def _scatter_add(tgt, idx, src, axis=0):
    return tgt.at[idx].add(src)

def _segment_sum(src, seg, n):
    return jax.ops.segment_sum(src, seg, n)
kernel_name = 'mk_prb_d1_jaxref_r8_59ca1d'

def setup_inputs(seed: int=0):
    np.random.seed(seed)
    _w = jnp.asarray

    def _L0_attn_setup():
        import jax, jax.numpy as jnp
        import numpy as np
        B, T, D = (4, 128, 128)
        H, KVH = (16, 4)
        HD = D // H
        DFF = 512
        WINDOW = 32
        EPS = 1e-05

        def _layernorm(x, g, b):
            mu = jnp.mean(x, axis=-1, keepdims=True)
            var = jnp.mean(jnp.square(x - mu), axis=-1, keepdims=True)
            return (x - mu) * jax.lax.rsqrt(var + EPS) * g + b

        def _rope(x):
            half = HD // 2
            theta = 1.0 / 10000.0 ** (jnp.arange(half, dtype=jnp.float32) / half)
            pos = jnp.arange(x.shape[2], dtype=jnp.float32)
            freqs = jnp.outer(pos, theta)
            cos_f, sin_f = (jnp.cos(freqs), jnp.sin(freqs))
            x1, x2 = (x[..., :half], x[..., half:])
            return jnp.concatenate([x1 * cos_f - x2 * sin_f, x2 * cos_f + x1 * sin_f], axis=-1)
        key = jax.random.key(seed)
        ks = jax.random.split(key, 16)
        s = 0.02
        d = {'x': jax.random.normal(ks[0], (B, T, D), dtype=jnp.float32), 'Wq': jax.random.normal(ks[1], (D, H * HD), dtype=jnp.float32) * s, 'bq': jnp.zeros((H * HD,), jnp.float32), 'Wk': jax.random.normal(ks[2], (D, KVH * HD), dtype=jnp.float32) * s, 'bk': jnp.zeros((KVH * HD,), jnp.float32), 'Wv': jax.random.normal(ks[3], (D, KVH * HD), dtype=jnp.float32) * s, 'bv': jnp.zeros((KVH * HD,), jnp.float32), 'Wo': jax.random.normal(ks[4], (D, D), dtype=jnp.float32) * s, 'bo': jnp.zeros((D,), jnp.float32), 'g1': jnp.ones((D,), jnp.float32), 'b1': jnp.zeros((D,), jnp.float32), 'Wf1': jax.random.normal(ks[5], (D, DFF), dtype=jnp.float32) * s, 'bf1': jnp.zeros((DFF,), jnp.float32), 'Wf2': jax.random.normal(ks[6], (DFF, D), dtype=jnp.float32) * s, 'bf2': jnp.zeros((D,), jnp.float32), 'g2': jnp.ones((D,), jnp.float32), 'b2': jnp.zeros((D,), jnp.float32)}
        return d
    _L0_attn_in = _L0_attn_setup()

    def _L0_ffn_setup():
        import jax, jax.numpy as jnp
        import numpy as np
        DIM = 128
        DEPTH = 2
        HEADS = 8
        DIM_HEAD = 64
        WINDOW = 64
        INNER = HEADS * DIM_HEAD
        HID = int(DIM * 4 * 2 / 3)
        B, N = (2, 1024)
        QK_SCALE = 8.0

        def shift_token(t):
            t1, t2 = jnp.split(t, 2, axis=-1)
            t2 = jnp.pad(t2, ((0, 0), (1, 0), (0, 0)))[:, :-1]
            return jnp.concatenate([t1, t2], axis=-1)

        def l2norm(t):
            return t / jnp.clip(jnp.linalg.norm(t, axis=-1, keepdims=True), 1e-12)

        def rotate_half(x):
            x1, x2 = jnp.split(x, 2, axis=-1)
            return jnp.concatenate([-x2, x1], axis=-1)

        def rotary_xpos(q, k):
            n = q.shape[-2]
            half_idx = jnp.arange(0, DIM_HEAD, 2, dtype=jnp.float32)
            inv_freq = 1.0 / 10000.0 ** (half_idx / DIM_HEAD)
            t = jnp.arange(n, dtype=jnp.float32)
            freqs = t[:, None] * inv_freq[None, :]
            freqs = jnp.concatenate([freqs, freqs], axis=-1)
            base = (half_idx + 0.4 * DIM_HEAD) / (1.4 * DIM_HEAD)
            power = (t - n // 2) / float(WINDOW // 2)
            scale = base[None, :] ** power[:, None]
            scale = jnp.concatenate([scale, scale], axis=-1)
            cos, sin = (jnp.cos(freqs), jnp.sin(freqs))
            q = q * cos * scale + rotate_half(q) * sin * scale
            k = k * cos / scale + rotate_half(k) * sin / scale
            return (q, k)

        def local_attention(q, k, v):
            b, h, n, d = q.shape
            w = n // WINDOW
            bq = q.reshape(b, h, w, WINDOW, d) * QK_SCALE
            bk = k.reshape(b, h, w, WINDOW, d)
            bv = v.reshape(b, h, w, WINDOW, d)

            def look_around(t):
                p = jnp.pad(t, ((0, 0), (0, 0), (1, 0), (0, 0), (0, 0)))
                return jnp.concatenate([p[:, :, :w], p[:, :, 1:]], axis=3)
            bk, bv = (look_around(bk), look_around(bv))
            bt = jnp.arange(n).reshape(w, WINDOW)
            btp = jnp.pad(bt, ((1, 0), (0, 0)), constant_values=-1)
            btk = jnp.concatenate([btp[:w], btp[1:]], axis=1)
            sim = jnp.einsum('bhwid,bhwjd->bhwij', bq, bk)
            i = bt[:, :, None]
            j = btk[:, None, :]
            mask = (i < j) | (i > j + WINDOW) | (j == -1)
            sim = jnp.where(mask, -jnp.finfo(sim.dtype).max, sim)
            attn = jax.nn.softmax(sim, axis=-1)
            out = jnp.einsum('bhwij,bhwjd->bhwid', attn, bv)
            return out.reshape(b, h, n, d)

        def _layer(x, wqkv, qs, ksc, wo, lg, lb, w1, b1, w2, b2):
            b, n, _ = x.shape
            h = shift_token(x)
            qkv = h @ wqkv
            q, k, v = jnp.split(qkv, 3, axis=-1)
            to_heads = lambda t: t.reshape(b, n, HEADS, DIM_HEAD).transpose(0, 2, 1, 3)
            q, k, v = (to_heads(q), to_heads(k), to_heads(v))
            q = l2norm(q) * qs
            k = l2norm(k) * ksc
            q, k = rotary_xpos(q, k)
            o = local_attention(q, k, v)
            o = o.transpose(0, 2, 1, 3).reshape(b, n, INNER)
            x = x + o @ wo
            h = shift_token(x)
            mu = h.mean(-1, keepdims=True)
            var = h.var(-1, keepdims=True)
            h = (h - mu) / jnp.sqrt(var + 1e-05) * lg + lb
            h = h @ w1 + b1
            a, g = jnp.split(h, 2, axis=-1)
            h = a * jax.nn.gelu(g, approximate=False)
            x = x + h @ w2 + b2
            return x
        key = jax.random.key(seed)
        ks = jax.random.split(key, 6)
        return {'x': jax.random.normal(ks[0], (B, N, DIM), jnp.float32), 'wqkv': jax.random.normal(ks[1], (DEPTH, DIM, 3 * INNER), jnp.float32) * 0.02, 'q_scale': jnp.ones((DEPTH, DIM_HEAD), jnp.float32), 'k_scale': jnp.ones((DEPTH, DIM_HEAD), jnp.float32), 'wo': jax.random.normal(ks[2], (DEPTH, INNER, DIM), jnp.float32) * 0.02, 'ln_g': jnp.ones((DEPTH, DIM), jnp.float32), 'ln_b': jnp.zeros((DEPTH, DIM), jnp.float32), 'w1': jax.random.normal(ks[3], (DEPTH, DIM, 2 * HID), jnp.float32) * 0.02, 'b1': jnp.zeros((DEPTH, 2 * HID), jnp.float32), 'w2': jax.random.normal(ks[4], (DEPTH, HID, DIM), jnp.float32) * 0.02, 'b2': jnp.zeros((DEPTH, DIM), jnp.float32)}
    _L0_ffn_in = _L0_ffn_setup()
    _d = {'L0_attn_x': _L0_attn_in['x'], 'L0_attn_Wq': _L0_attn_in['Wq'], 'L0_attn_bq': _L0_attn_in['bq'], 'L0_attn_Wk': _L0_attn_in['Wk'], 'L0_attn_bk': _L0_attn_in['bk'], 'L0_attn_Wv': _L0_attn_in['Wv'], 'L0_attn_bv': _L0_attn_in['bv'], 'L0_attn_Wo': _L0_attn_in['Wo'], 'L0_attn_bo': _L0_attn_in['bo'], 'L0_attn_g1': _L0_attn_in['g1'], 'L0_attn_b1': _L0_attn_in['b1'], 'L0_attn_Wf1': _L0_attn_in['Wf1'], 'L0_attn_bf1': _L0_attn_in['bf1'], 'L0_attn_Wf2': _L0_attn_in['Wf2'], 'L0_attn_bf2': _L0_attn_in['bf2'], 'L0_attn_g2': _L0_attn_in['g2'], 'L0_attn_b2': _L0_attn_in['b2'], 'L0_ffn_wqkv': _L0_ffn_in['wqkv'], 'L0_ffn_q_scale': _L0_ffn_in['q_scale'], 'L0_ffn_k_scale': _L0_ffn_in['k_scale'], 'L0_ffn_wo': _L0_ffn_in['wo'], 'L0_ffn_ln_g': _L0_ffn_in['ln_g'], 'L0_ffn_ln_b': _L0_ffn_in['ln_b'], 'L0_ffn_w1': _L0_ffn_in['w1'], 'L0_ffn_b1': _L0_ffn_in['b1'], 'L0_ffn_w2': _L0_ffn_in['w2'], 'L0_ffn_b2': _L0_ffn_in['b2']}
    _x0 = _d['L0_attn_x']
    _d['L0_attn_x'] = jax.random.normal(jax.random.fold_in(jax.random.key(seed), 1), (4, 1024, 128), dtype=_x0.dtype)
    del _x0
    return _d

def reference(L0_attn_x, L0_attn_Wq, L0_attn_bq, L0_attn_Wk, L0_attn_bk, L0_attn_Wv, L0_attn_bv, L0_attn_Wo, L0_attn_bo, L0_attn_g1, L0_attn_b1, L0_attn_Wf1, L0_attn_bf1, L0_attn_Wf2, L0_attn_bf2, L0_attn_g2, L0_attn_b2, L0_ffn_wqkv, L0_ffn_q_scale, L0_ffn_k_scale, L0_ffn_wo, L0_ffn_ln_g, L0_ffn_ln_b, L0_ffn_w1, L0_ffn_b1, L0_ffn_w2, L0_ffn_b2):

    def _L0_attn_ref(x, Wq, bq, Wk, bk, Wv, bv, Wo, bo, g1, b1, Wf1, bf1, Wf2, bf2, g2, b2):
        import jax, jax.numpy as jnp
        import numpy as np
        B, T, D = (4, 128, 128)
        H, KVH = (16, 4)
        HD = D // H
        DFF = 512
        WINDOW = 32
        EPS = 1e-05

        def _layernorm(x, g, b):
            mu = jnp.mean(x, axis=-1, keepdims=True)
            var = jnp.mean(jnp.square(x - mu), axis=-1, keepdims=True)
            return (x - mu) * jax.lax.rsqrt(var + EPS) * g + b

        def _rope(x):
            half = HD // 2
            theta = 1.0 / 10000.0 ** (jnp.arange(half, dtype=jnp.float32) / half)
            pos = jnp.arange(x.shape[2], dtype=jnp.float32)
            freqs = jnp.outer(pos, theta)
            cos_f, sin_f = (jnp.cos(freqs), jnp.sin(freqs))
            x1, x2 = (x[..., :half], x[..., half:])
            return jnp.concatenate([x1 * cos_f - x2 * sin_f, x2 * cos_f + x1 * sin_f], axis=-1)
        Bt, Tt, _ = x.shape
        h = _layernorm(x, g1, b1)
        q = (h @ Wq + bq).reshape(Bt, Tt, H, HD).transpose(0, 2, 1, 3)
        k = (h @ Wk + bk).reshape(Bt, Tt, KVH, HD).transpose(0, 2, 1, 3)
        v = (h @ Wv + bv).reshape(Bt, Tt, KVH, HD).transpose(0, 2, 1, 3)
        group = H // KVH
        k = jnp.repeat(k, group, axis=1)
        v = jnp.repeat(v, group, axis=1)
        q, k = (_rope(q), _rope(k))
        scores = jnp.einsum('bhqd,bhkd->bhqk', q, k) / jnp.sqrt(jnp.float32(HD))
        row = jnp.arange(Tt)[:, None]
        col = jnp.arange(Tt)[None, :]
        valid = (col <= row) & (row - col < WINDOW)
        scores = jnp.where(valid, scores, jnp.float32(-1000000000.0))
        attn = jax.nn.softmax(scores, axis=-1)
        out = jnp.einsum('bhqk,bhkd->bhqd', attn, v)
        out = out.transpose(0, 2, 1, 3).reshape(Bt, Tt, D)
        x = x + (out @ Wo + bo)
        h2 = _layernorm(x, g2, b2)
        ff = jax.nn.gelu(h2 @ Wf1 + bf1, approximate=False) @ Wf2 + bf2
        return x + ff

    def _L0_ffn_ref(x, wqkv, q_scale, k_scale, wo, ln_g, ln_b, w1, b1, w2, b2):
        import jax, jax.numpy as jnp
        import numpy as np
        DIM = 128
        DEPTH = 2
        HEADS = 8
        DIM_HEAD = 64
        WINDOW = 64
        INNER = HEADS * DIM_HEAD
        HID = int(DIM * 4 * 2 / 3)
        B, N = (2, 1024)
        QK_SCALE = 8.0

        def shift_token(t):
            t1, t2 = jnp.split(t, 2, axis=-1)
            t2 = jnp.pad(t2, ((0, 0), (1, 0), (0, 0)))[:, :-1]
            return jnp.concatenate([t1, t2], axis=-1)

        def l2norm(t):
            return t / jnp.clip(jnp.linalg.norm(t, axis=-1, keepdims=True), 1e-12)

        def rotate_half(x):
            x1, x2 = jnp.split(x, 2, axis=-1)
            return jnp.concatenate([-x2, x1], axis=-1)

        def rotary_xpos(q, k):
            n = q.shape[-2]
            half_idx = jnp.arange(0, DIM_HEAD, 2, dtype=jnp.float32)
            inv_freq = 1.0 / 10000.0 ** (half_idx / DIM_HEAD)
            t = jnp.arange(n, dtype=jnp.float32)
            freqs = t[:, None] * inv_freq[None, :]
            freqs = jnp.concatenate([freqs, freqs], axis=-1)
            base = (half_idx + 0.4 * DIM_HEAD) / (1.4 * DIM_HEAD)
            power = (t - n // 2) / float(WINDOW // 2)
            scale = base[None, :] ** power[:, None]
            scale = jnp.concatenate([scale, scale], axis=-1)
            cos, sin = (jnp.cos(freqs), jnp.sin(freqs))
            q = q * cos * scale + rotate_half(q) * sin * scale
            k = k * cos / scale + rotate_half(k) * sin / scale
            return (q, k)

        def local_attention(q, k, v):
            b, h, n, d = q.shape
            w = n // WINDOW
            bq = q.reshape(b, h, w, WINDOW, d) * QK_SCALE
            bk = k.reshape(b, h, w, WINDOW, d)
            bv = v.reshape(b, h, w, WINDOW, d)

            def look_around(t):
                p = jnp.pad(t, ((0, 0), (0, 0), (1, 0), (0, 0), (0, 0)))
                return jnp.concatenate([p[:, :, :w], p[:, :, 1:]], axis=3)
            bk, bv = (look_around(bk), look_around(bv))
            bt = jnp.arange(n).reshape(w, WINDOW)
            btp = jnp.pad(bt, ((1, 0), (0, 0)), constant_values=-1)
            btk = jnp.concatenate([btp[:w], btp[1:]], axis=1)
            sim = jnp.einsum('bhwid,bhwjd->bhwij', bq, bk)
            i = bt[:, :, None]
            j = btk[:, None, :]
            mask = (i < j) | (i > j + WINDOW) | (j == -1)
            sim = jnp.where(mask, -jnp.finfo(sim.dtype).max, sim)
            attn = jax.nn.softmax(sim, axis=-1)
            out = jnp.einsum('bhwij,bhwjd->bhwid', attn, bv)
            return out.reshape(b, h, n, d)

        def _layer(x, wqkv, qs, ksc, wo, lg, lb, w1, b1, w2, b2):
            b, n, _ = x.shape
            h = shift_token(x)
            qkv = h @ wqkv
            q, k, v = jnp.split(qkv, 3, axis=-1)
            to_heads = lambda t: t.reshape(b, n, HEADS, DIM_HEAD).transpose(0, 2, 1, 3)
            q, k, v = (to_heads(q), to_heads(k), to_heads(v))
            q = l2norm(q) * qs
            k = l2norm(k) * ksc
            q, k = rotary_xpos(q, k)
            o = local_attention(q, k, v)
            o = o.transpose(0, 2, 1, 3).reshape(b, n, INNER)
            x = x + o @ wo
            h = shift_token(x)
            mu = h.mean(-1, keepdims=True)
            var = h.var(-1, keepdims=True)
            h = (h - mu) / jnp.sqrt(var + 1e-05) * lg + lb
            h = h @ w1 + b1
            a, g = jnp.split(h, 2, axis=-1)
            h = a * jax.nn.gelu(g, approximate=False)
            x = x + h @ w2 + b2
            return x
        for l in range(DEPTH):
            x = _layer(x, wqkv[l], q_scale[l], k_scale[l], wo[l], ln_g[l], ln_b[l], w1[l], b1[l], w2[l], b2[l])
        return x
    x = L0_attn_x
    xn = _layernorm(x, axis=-1)
    x = x + _L0_attn_ref(xn, L0_attn_Wq, L0_attn_bq, L0_attn_Wk, L0_attn_bk, L0_attn_Wv, L0_attn_bv, L0_attn_Wo, L0_attn_bo, L0_attn_g1, L0_attn_b1, L0_attn_Wf1, L0_attn_bf1, L0_attn_Wf2, L0_attn_bf2, L0_attn_g2, L0_attn_b2) + _L0_ffn_ref(xn, L0_ffn_wqkv, L0_ffn_q_scale, L0_ffn_k_scale, L0_ffn_wo, L0_ffn_ln_g, L0_ffn_ln_b, L0_ffn_w1, L0_ffn_b1, L0_ffn_w2, L0_ffn_b2)
    return x

_drawn_inputs = setup_inputs


def setup_inputs(seed=0):
    import zlib

    import numpy as np

    out = dict(_drawn_inputs(seed))
    spreads = {'L0_attn_bq': (0.0, 0.8),
     'L0_attn_bk': (0.0, 2.0),
     'L0_attn_bv': (0.0, 0.797),
     'L0_attn_bo': (0.0, 2.0),
     'L0_attn_g1': (1.0, 0.6),
     'L0_attn_b1': (0.0, 0.8),
     'L0_attn_bf1': (0.0, 2.0),
     'L0_attn_bf2': (0.0, 2.0),
     'L0_attn_g2': (1.0, 0.6),
     'L0_attn_b2': (0.0, 2.0),
     'L0_ffn_q_scale': (1.0, 0.6),
     'L0_ffn_k_scale': (1.0, 0.6),
     'L0_ffn_ln_g': (1.0, 0.6),
     'L0_ffn_ln_b': (0.0, 0.8),
     'L0_ffn_b1': (0.0, 0.8),
     'L0_ffn_b2': (0.0, 0.753)}
    factors = {'L0_attn_Wq': 8.0,
     'L0_attn_Wk': 8.0,
     'L0_attn_Wv': 8.0,
     'L0_attn_Wo': 5.494,
     'L0_attn_Wf1': 8.623,
     'L0_attn_Wf2': 2.879,
     'L0_ffn_wqkv': 5.967,
     'L0_ffn_wo': 5.924,
     'L0_ffn_w1': 8.0,
     'L0_ffn_w2': 8.0}
    for name, (base, spread) in spreads.items():
        noise = np.random.default_rng([zlib.crc32(name.encode()), seed]).standard_normal(out[name].shape)
        drawn = base * np.exp(spread * noise) if base else spread * noise
        out[name] = jnp.asarray(drawn.astype(out[name].dtype))
    for name, factor in factors.items():
        out[name] = (out[name] * factor).astype(out[name].dtype)
    return out
```

```python
from contextlib import ExitStack

import concourse.bass as bass
from concourse import mybir

F32 = mybir.dt.float32
BF16 = mybir.dt.bfloat16
I32 = mybir.dt.int32
ALU = mybir.AluOpType
ACT = mybir.ActivationFunctionType
AX_X = mybir.AxisListType.X

P = 128
BATCH, T, D = 4, 1024, 128
TILES = T // P
CH = 512
CHUNKS = T // CH
TPC = CH // P
LAYERS = 2
A_KV, A_GRP, A_HD, A_WIN, A_FF = 4, 4, 8, 32, 4
B_H, B_HD, B_WIN = 8, 64, 64
B_QK = 2 * B_H * B_HD // P
HID = 341
HID_T = [(0, 128), (128, 128), (256, HID - 256)]
EPS = 1e-5

A_UNITS = TILES * A_KV
B_UNITS = TILES * B_H // 4
UNITS = A_UNITS + LAYERS * B_UNITS

WA_Q, WA_QR, WA_K, WA_KR, WA_V = 0, 512, 1024, 1152, 1280
WA_N = 1312
(V_G1, V_B1, V_G2, V_B2, V_BO, V_BF2, V_BVR, V_BQ, V_BQR, V_BK, V_BKR, V_BF1) = (0, 1, 2, 3, 4, 5, 6, 7, 11, 15, 16, 17)
V_L = 21
(VL_G, VL_B, VL_B2, VL_QS, VL_B1) = (0, 1, 2, 3, 7)
VL_N = 13
V_N = V_L + LAYERS * VL_N

STAGES = [("in", 4), ("a_proj", 21), ("a_wo", 2), ("a_ln", 4), ("a_ffn", 10)]
for _l in range(LAYERS):
    STAGES += [(f"proj{_l}", 40), (f"norm{_l}", 16), (f"wo{_l}", 2), (f"ln{_l}", 4), (f"ffn{_l}", 14)]
STAGES += [("out", 2)]
USE0 = {}
_n = 0
for _name, _k in STAGES:
    USE0[_name] = _n
    _n += _k
RING = 4


def unit(n):
    if n < A_UNITS:
        return -1, n // A_KV, n % A_KV
    m = n - A_UNITS
    return m // B_UNITS, m % B_UNITS // 2, m % 2


def program(nc, x, wa, wo, wf1, wf2, wvr, vec, wb, wob, w1, w2, tabs, ident, center, ones, cbf, out):
    ctx = ExitStack()
    with ctx:
        def sb(name, shape, dt=F32):
            return ctx.enter_context(nc.sbuf_tensor(name, shape, dt))

        def sem(name):
            return ctx.enter_context(nc.semaphore(name))

        wa_s = sb("wa_s", [P, WA_N])
        wo_s = sb("wo_s", [P, D])
        wf1_s = sb("wf1_s", [P, A_FF * P])
        wf2_s = sb("wf2_s", [P, A_FF, P])
        vec_s = sb("vec_s", [P, V_N])
        bias = sb("bias", [P, V_N])
        wb_s = sb("wb_s", [P, LAYERS, 2560])
        wob_s = sb("wob_s", [P, LAYERS, 4, P])
        w1_s = sb("w1_s", [P, LAYERS, 2 * HID])
        w2_s = sb("w2_s", [P, LAYERS, 3, P])
        tab_s = sb("tab_s", [P, 6, T])
        ident_s = sb("ident_s", [P, P])
        center_s = sb("center_s", [P, P])
        ones_s = sb("ones_s", [P, P + 2])
        eps_s = sb("eps_s", [P, 1])
        CB = cbf.shape[1]
        cbf_s = sb("cbf_s", [P, CB], BF16)
        o = 0
        identb = cbf_s[:, 0:128]
        o = 128
        smask = {-1: cbf_s[:, o:o + 320], 0: cbf_s[:, o + 320:o + 704]}
        o += 704
        smask0 = {-1: cbf_s[:, o:o + 256], 0: cbf_s[:, o + 256:o + 512]}
        o += 512
        tmask = {-1: cbf_s[:, o:o + 512], 0: cbf_s[:, o + 512:o + 1024]}
        o += 1024
        cmask = {-1: cbf_s[:, o:o + 128], 0: cbf_s[:, o + 128:o + 384]}
        o += 384
        selm = cbf_s[:, o:o + 512]
        o += 512
        seln = cbf_s[0:48, o:o + 1024]
        o += 1024
        assert o == CB

        x_tok = sb("x_tok", [P, TILES, D])
        xT = sb("xT", [P, T + 1])
        aT = sb("aT", [P, T])
        hT = sb("hT", [P, T])
        qk = sb("qk", [P, B_QK, T])
        vB = sb("vB", [P, TILES, B_H, B_HD + 1])
        vA = sb("vA", [P, TILES, A_KV, A_HD + 1])
        rt_tab = sb("rt_tab", [P, 4, T])
        oT = sb("oT", [P, 4, T])
        o_tok = sb("o_tok", [P, 2, 512])
        raw = sb("raw", [P, 2, CH])
        sq = sb("sq", [P, 2, CH])
        pc = sb("pc", [P, 2, CH])
        ps_ = sb("ps_", [P, 2, CH])
        pm = sb("pm", [P, 2, 512])
        pcor = sb("pcor", [P, 2, 256])
        gel = pm
        stat = sb("stat", [P, 12])
        mv = sb("mv", [P, 4])
        nw = sb("nw", [P, 4, 64])
        rsp = sb("rsp", [P, 2, TPC, 48], BF16)
        rT = sb("rT", [48, 2, CH], BF16)
        mx = sb("mx", [P, 2, 4])
        negm = sb("negm", [P, 2, 8], BF16)
        mT = sb("mT", [P, 2, P], BF16)
        rl = sb("rl", [P, 4])

        bank = ctx.enter_context(nc.psum_tensor("bank", [P, 8, 512], F32))
        s_bank = [bank[:, 0:2, :], bank[:, 2:4, :]]
        t_bank, c_bank, o_bank, x_bank = (bank[:, b, :] for b in (4, 5, 6, 7))

        s_load = sem("weights_loaded")
        setup_v = sem("setup_vector")
        setup_p = sem("setup_pool")
        setup_mm = sem("setup_products")
        first = s_load.num
        x_in = sem("x_loaded")
        tok_norm = sem("tokens_normed")
        mm_full = sem("product_ready")
        drained = [sem(f"bank{b}_drained") for b in range(RING)]
        raw_rdy = sem("raw_copied")
        prod_rdy = sem("rotary_products")
        sum_rdy = sem("rotated")
        ss_done = sem("squares_summed")
        rsp_rdy = sem("norms_split")
        rt_full = sem("norms_turned")
        rt_rdy = sem("norms_copied")
        shift_rdy = sem("shifted")
        sc_full = sem("scores_ready")
        max_rdy = sem("maxima_ready")
        mt_full = sem("maxima_turned")
        mt_rdy = sem("maxima_copied")
        st_full = sem("key_scores_ready")
        exp_done = sem("probs_ready")
        pv_done = sem("values_weighted")
        on_rdy = sem("heads_normalised")
        ot_full = sem("heads_turned")
        ot_rdy = sem("heads_copied")
        rstd_rdy = sem("rstd_ready")
        hn_rdy = sem("ln_ready")
        fin_rdy = sem("branches_added")
        out_rdy = sem("out_ready")
        out_done = sem("out_stored")
        v_link = sem("vector_step")
        last = v_link.num

        def xc(c):
            return xT[:, 1 + c * CH:1 + (c + 1) * CH]

        def cc(c):
            return slice(c * CH, (c + 1) * CH)

        biases = [(wa_s[:, WA_Q + j * P:WA_Q + (j + 1) * P], V_B1, V_BQ + j) for j in range(4)]
        biases += [(wa_s[:, WA_QR + j * P:WA_QR + (j + 1) * P], V_B1, V_BQR + j) for j in range(4)]
        biases += [(wa_s[:, WA_K:WA_K + P], V_B1, V_BK), (wa_s[:, WA_KR:WA_KR + P], V_B1, V_BKR)]
        biases += [(wf1_s[:, f * P:(f + 1) * P], V_B2, V_BF1 + f) for f in range(4)]
        for l in range(LAYERS):
            for half in range(2):
                for f, (s, w) in enumerate(HID_T):
                    biases.append((w1_s[:, l, half * HID + s:half * HID + s + w], V_L + l * VL_N + VL_B,
                                   V_L + l * VL_N + VL_B1 + half * 3 + f))
        NB = len(biases)
        wvr_s = aT[:, 0:P]

        with nc.Block() as block:
            @block.sync
            def _(sp):
                for dst, src in ((wa_s[:, :], wa), (vec_s[:, :], vec), (wo_s[:, :], wo), (wf1_s[:, :], wf1),
                                 (wf2_s[:, :, :], wf2), (wvr_s, wvr), (w1_s[:, :, :], w1),
                                 (wb_s[:, :, :], wb), (tab_s[:, :, :], tabs)):
                    sp.dma_start(dst, src).then_inc(s_load, 16)

            @block.scalar
            def _(act):
                for dst, src in ((ident_s[:, :], ident), (center_s[:, :], center), (ones_s[:, :], ones),
                                 (cbf_s[:, :], cbf), (wob_s[:, :, :, :], wob), (w2_s[:, :, :, :], w2)):
                    act.dma_start(dst, src).then_inc(s_load, 16)

            @block.gpsimd
            def _(pool):
                pool.memset(vB[:, :, :, B_HD:B_HD + 1], 1.0).then_inc(setup_p, 1)
                pool.memset(vA[:, :, :, A_HD:A_HD + 1], 1.0).then_inc(setup_p, 1)
                pool.memset(xT[:, 0:1], 0.0).then_inc(setup_p, 1)
                pool.memset(eps_s[:, :], EPS).then_inc(setup_p, 1)
                pool.memset(mT[:, :, :], 0.0).then_inc(setup_p, 1)

            @block.tensor
            def _(pe):
                pe.wait_ge(s_load, 15 * 16)
                for n, (w, b, _) in enumerate(biases):
                    pe.matmul(bank[0:w.shape[1], 0, n:n + 1], w, vec_s[:, b:b + 1], start=True, stop=True)
                pe.matmul(bank[:, 0, NB:NB + 1], wvr_s, vec_s[:, V_B1:V_B1 + 1],
                          start=True, stop=True).then_inc(setup_mm, 1)
                pe.wait_ge(setup_v, 1)
                pe.matmul(bank[:, 1, 0:1], wo_s[:, :], bias[:, V_BVR:V_BVR + 1],
                          start=True, stop=True).then_inc(setup_mm, 1)

            @block.vector
            def _(dve):
                dve.wait_ge(s_load, 15 * 16)
                dve.wait_ge(setup_mm, 1)
                dve.tensor_tensor(bias[:, V_BVR:V_BVR + 1], bank[:, 0, NB:NB + 1], vec_s[:, V_BVR:V_BVR + 1],
                                  ALU.add).then_inc(setup_v, 1)
                for n, (w, _, dst) in enumerate(biases):
                    m = w.shape[1]
                    dve.tensor_tensor(bias[0:m, dst:dst + 1], bank[0:m, 0, n:n + 1], vec_s[0:m, dst:dst + 1],
                                      ALU.add).then_inc(setup_v, 1)
                dve.tensor_scalar(wa_s[:, :], wa_s[:, :], vec_s[:, V_G1:V_G1 + 1], None, ALU.mult).then_inc(setup_v, 1)
                dve.tensor_scalar(wf1_s[:, :], wf1_s[:, :], vec_s[:, V_G2:V_G2 + 1], None,
                                  ALU.mult).then_inc(setup_v, 1)
                for l in range(LAYERS):
                    g = V_L + l * VL_N + VL_G
                    dve.tensor_scalar(w1_s[:, l, :], w1_s[:, l, :], vec_s[:, g:g + 1], None,
                                      ALU.mult).then_inc(setup_v, 1)
                dve.wait_ge(setup_mm, 2)
                dve.tensor_tensor(bias[:, V_BO:V_BO + 1], bank[:, 1, 0:1], vec_s[:, V_BO:V_BO + 1],
                                  ALU.add).then_inc(setup_v, 1)

        def pair(br, c, k):
            return c * 5 + k if br < 0 else 10 + br * 16 + c * 8 + k

        def tile_of(n):
            return unit(n)[1]

        def taken(eng, i):
            eng.wait_ge(drained[i % RING], i // RING + 1)

        def use_wait(eng, i):
            if i >= RING:
                eng.wait_ge(drained[i % RING], i // RING)

        rt_tok, h_tok = (rt_tab[:, r, :].rearrange("p (t d) -> p t d", d=D) for r in range(2))

        def ln_n(name, c):
            return {"a_ln": 0, "ln0": 1, "ln1": 2}[name] * CHUNKS + c

        def values_use(br, t):
            return USE0["a_proj"] + 20 if br < 0 else USE0[f"proj{br}"] + t // TPC * 20 + 16 + t % TPC

        LAST_UNIT = {-1: A_UNITS - 1, 0: A_UNITS + B_UNITS - 1, 1: UNITS - 1}
        FIRST_UNIT = {-1: 0, 0: A_UNITS, 1: A_UNITS + B_UNITS}
        def ot_n(br, t):
            return (br + 1) * TILES + t

        with nc.Fori(0, BATCH) as b:
            with nc.Block() as block:
                x_b = x[bass.ds(b, 1), :, :].rearrange("a (t p) d -> p (a t) d", p=P)
                out_b = out[bass.ds(b, 1), :, :].rearrange("a (t p) d -> p (a t) d", p=P)

                @block.sync
                def _(sp):
                    sp.dma_start(x_tok[:, :, :], x_b).then_inc(x_in, 16)
                    for c in range(CHUNKS):
                        sp.wait_ge(out_rdy, c + 1)
                        sp.dma_start(out_b[:, c * TPC:(c + 1) * TPC, :],
                                     x_tok[:, c * TPC:(c + 1) * TPC, :]).then_inc(out_done, 16)
                    sp.wait_ge(out_done, 16 * CHUNKS)

                @block.gpsimd
                def _(pool):
                    for br in (-1, 0, 1):
                        for c in range(CHUNKS):
                            for k in range(5 if br < 0 else B_QK):
                                j = pair(br, c, k)
                                if br < 0:
                                    taken(pool, USE0["a_proj"] + c * 10 + 2 * k)
                                    taken(pool, USE0["a_proj"] + c * 10 + 2 * k + 1)
                                else:
                                    pool.wait_ge(prod_rdy, j - 10 + 1)
                                    taken(pool, USE0[f"proj{br}"] + c * 20 + 2 * k + 1)
                                if br >= 0 and c == 0 and k == 0:
                                    pool.wait_ge(st_full, FIRST_UNIT[br])
                                pool.tensor_tensor(qk[:, k, cc(c)], pc[:, j % 2, :], ps_[:, j % 2, :],
                                                   ALU.add).then_inc(sum_rdy, 1)

                @block.tensor
                def _(pe):
                    def product(i, parts, signal=True):
                        use_wait(pe, i)
                        m = parts[0][0].shape[1]
                        n = parts[0][1].shape[1]
                        for q, (lhs, rhs) in enumerate(parts):
                            mm = pe.matmul(bank[0:m, i % RING, 0:n], lhs, rhs, start=(q == 0),
                                           stop=(q == len(parts) - 1))
                        mm.then_inc(mm_full, 1)

                    def scores(n):
                        br, t, g = unit(n)
                        A = br < 0
                        w = P if t == 0 else P + (A_WIN if A else B_WIN)
                        if n - FIRST_UNIT[br] >= 2:
                            pe.wait_ge(max_rdy, n - 1)
                        elif n - FIRST_UNIT[br] == 0:
                            stop = USE0["a_wo"] if A else USE0[f"wo{br}"]
                            for i in range(stop - RING, stop):
                                taken(pe, i)
                        if A:
                            pe.wait_ge(sum_rdy, pair(br, t // TPC, 4) + 1)
                        else:
                            for k in range(B_QK - RING, B_QK):
                                taken(pe, USE0[f"norm{br}"] + t // TPC * B_QK + k)
                        mask = (smask0 if t == 0 else smask)[min(br, 0)]
                        q0, k0 = t * P, (t + 1) * P - w
                        for h in range(4):
                            dst = s_bank[n % 2][:, h // 2, :]
                            if h % 2 == 0:
                                pe.matmul(dst[:, 0:2 * w], identb, mask, start=True, stop=False,
                                          skip_group_check=True)
                            if A:
                                mm = pe.matmul(dst[:, (h % 2) * w:(h % 2 + 1) * w], qk[32 * g:32 * g + 8, h, q0:q0 + P],
                                          qk[32 * g:32 * g + 8, 4, k0:k0 + w], start=False, stop=(h % 2 == 1),
                                          skip_group_check=True)
                            else:
                                r = slice(64 * g, 64 * g + 64)
                                mm = pe.matmul(dst[:, (h % 2) * w:(h % 2 + 1) * w], qk[r, h, q0:q0 + P],
                                               qk[r, 4 + h, k0:k0 + w], start=False, stop=(h % 2 == 1),
                                               skip_group_check=True)
                        mm.then_inc(sc_full, 1)

                    def turn_max(n):
                        pe.wait_ge(max_rdy, n + 1)
                        if n >= 1:
                            pe.wait_ge(mt_rdy, n)
                        if ot_before(n):
                            pe.wait_ge(ot_rdy, ot_before(n))
                        pe.transpose(x_bank[0:8, 0:64].bitcast(BF16), negm[:, n % 2, :], identb).then_inc(mt_full, 1)

                    def ot_before(n):
                        br, t, g = unit(n)
                        per = A_KV if br < 0 else 2
                        done = t - (1 if g == 0 else 0)
                        return (br + 1) * TILES + max(done, 0)

                    def key_scores(n):
                        br, t, g = unit(n)
                        A = br < 0
                        win = A_WIN if A else B_WIN
                        pe.wait_ge(mt_rdy, n + 1)
                        if n >= 1:
                            pe.wait_ge(exp_done, n)
                        q0 = t * P
                        e = slice(P - win, P)
                        rows = slice(32 * g, 32 * g + 8) if A else slice(64 * g, 64 * g + 64)
                        pe.matmul(t_bank, identb, tmask[min(br, 0)], start=True, stop=False, skip_group_check=True)
                        for h in range(4):
                            pe.matmul(t_bank[:, h * P:(h + 1) * P], selm[:, h * P:(h + 1) * P], mT[:, n % 2, :],
                                      start=False, stop=False, skip_group_check=True)
                        if t:
                            pe.matmul(c_bank[e, 0:4 * win], identb[:, e], cmask[min(br, 0)],
                                      start=True, stop=False, skip_group_check=True)
                            for h in range(4):
                                pe.matmul(c_bank[e, h * win:(h + 1) * win], selm[:, h * P:h * P + win],
                                          mT[:, n % 2, 0:win], start=False, stop=False, skip_group_check=True)
                            for h in range(4):
                                pe.matmul(c_bank[e, h * win:(h + 1) * win], qk[rows, 4 if A else 4 + h, q0 - win:q0],
                                          qk[rows, h, q0:q0 + win], start=False, stop=(h == 3),
                                          skip_group_check=True)
                        for h in range(4):
                            mm = pe.matmul(t_bank[:, h * P:(h + 1) * P], qk[rows, 4 if A else 4 + h, q0:q0 + P],
                                           qk[rows, h, q0:q0 + P], start=False, stop=(h == 3),
                                           skip_group_check=True)
                        mm.then_inc(st_full, 1)

                    def weigh(n):
                        br, t, g = unit(n)
                        A = br < 0
                        win, hd = (A_WIN, A_HD) if A else (B_WIN, B_HD)
                        pe.wait_ge(exp_done, n + 1)
                        if n >= 1:
                            pe.wait_ge(on_rdy, n)
                        taken(pe, values_use(br, t))
                        dst = [slice(h * (hd + 1), (h + 1) * (hd + 1)) for h in range(4)]
                        for h in range(4):
                            v = (vA[:, t, g, :] if A else vB[:, t, 2 * h + g, :])
                            mm = pe.matmul(o_bank[:, dst[h]], pm[:, n % 2, h * P:(h + 1) * P], v, start=(h == 0),
                                           stop=(t == 0), skip_group_check=True)
                        if t:
                            for h in range(4):
                                e = slice(P - win, P)
                                v = (vA[e, t - 1, g, :] if A else vB[e, t - 1, 2 * h + g, :])
                                mm = pe.matmul(o_bank[0:win, dst[h]], pcor[e, n % 2, h * win:(h + 1) * win], v,
                                               start=False, stop=True, skip_group_check=True)
                        mm.then_inc(pv_done, 1)
                        if g == (A_KV - 1 if A else 1):
                            pe.wait_ge(on_rdy, n + 1)
                            pe.wait_ge(mt_rdy, min(n + 2, LAST_UNIT[br] + 1))
                            for f in range(1 if A else 4):
                                mm = pe.transpose(x_bank[:, f * P:(f + 1) * P], o_tok[:, t % 2, f * P:(f + 1) * P],
                                                  ident_s[:, :])
                            mm.then_inc(ot_full, 1)

                    def attention(br):
                        n0, n1 = FIRST_UNIT[br], LAST_UNIT[br]
                        scores(n0)
                        for n in range(n0, n1 + 1):
                            if n < n1:
                                scores(n + 1)
                            turn_max(n)
                            if n > n0:
                                weigh(n - 1)
                            key_scores(n)
                        weigh(n1)

                    def layernorm(name, src, ready):
                        u = USE0[name]
                        for c in range(CHUNKS):
                            ready(c)
                            product(u + c, [(center_s[:, :], src(c))])
                        for c in range(CHUNKS):
                            taken(pe, u + c)
                            product(u + CHUNKS + c, [(ones_s[:, 0:P], sq[:, c, :])])

                    for c in range(CHUNKS):
                        for w, src in enumerate((None, h_tok)):
                            i = USE0["in"] + 2 * c + w
                            use_wait(pe, i)
                            pe.wait_ge(tok_norm, (c + 1) * TPC if w == 0 else TILES + (c + 1) * TPC)
                            for tt in range(TPC):
                                t = c * TPC + tt
                                tok = (rt_tok if w == 0 else h_tok)[:, t, :]
                                mm = pe.transpose(bank[:, i % RING, tt * P:(tt + 1) * P], tok, ident_s[:, :])
                            mm.then_inc(mm_full, 1)
                    u = USE0["a_proj"]
                    for c in range(CHUNKS):
                        taken(pe, USE0["in"] + 2 * c + 1)
                        for k in range(5):
                            w0 = WA_Q + k * P if k < 4 else WA_K
                            w1_ = WA_QR + k * P if k < 4 else WA_KR
                            product(u + c * 10 + 2 * k, [(wa_s[:, w0:w0 + P], hT[:, cc(c)])])
                            product(u + c * 10 + 2 * k + 1, [(wa_s[:, w1_:w1_ + P], hT[:, cc(c)])])
                    use_wait(pe, u + 20)
                    for t in range(TILES):
                        mm = pe.matmul(bank[:, (u + 20) % RING, t * 32:(t + 1) * 32], hT[:, t * P:(t + 1) * P],
                                       wa_s[:, WA_V:WA_V + 32], start=True, stop=True)
                    mm.then_inc(mm_full, 1)
                    attention(-1)
                    for c in range(CHUNKS):
                        pe.wait_ge(ot_rdy, (c + 1) * TPC)
                        product(USE0["a_wo"] + c, [(wo_s[:, :], oT[:, 0, cc(c)])])
                    layernorm("a_ln", lambda c: aT[:, cc(c)], lambda c: taken(pe, USE0["a_wo"] + c))
                    u = USE0["a_ffn"]
                    for c in range(CHUNKS):
                        pe.wait_ge(hn_rdy, c + 1)
                        for f in range(4):
                            product(u + c * 5 + f, [(wf1_s[:, f * P:(f + 1) * P], hT[:, cc(c)])])
                        for f in range(4):
                            taken(pe, u + c * 5 + f)
                        product(u + c * 5 + 4, [(wf2_s[:, f, :], oT[:, f, cc(c)]) for f in range(4)])

                    for l in range(LAYERS):
                        u = USE0[f"proj{l}"]

                        def sum_squares(c, k):
                            i = u + c * 20 + 2 * k
                            j = pair(l, c, k)
                            taken(pe, i)
                            for tt in range(TPC):
                                mm = pe.matmul(bank[:, 4 + c, tt * 16 + 2 * k:tt * 16 + 2 * k + 2],
                                               sq[:, j % 2, tt * P:(tt + 1) * P], ones_s[:, P:P + 2],
                                               start=True, stop=True)
                            mm.then_inc(ss_done, 1)

                        for c in range(CHUNKS):
                            pe.wait_ge(shift_rdy, l * 4 + c + 1)
                            for k in range(B_QK):
                                product(u + c * 20 + 2 * k, [(wb_s[:, l, k * P:(k + 1) * P], hT[:, cc(c)])])
                                product(u + c * 20 + 2 * k + 1,
                                        [(wb_s[:, l, 1024 + k * P:1024 + (k + 1) * P], hT[:, cc(c)])])
                                if k:
                                    sum_squares(c, k - 1)
                            for tt in range(TPC):
                                t = c * TPC + tt
                                product(u + c * 20 + 16 + tt, [(hT[:, t * P:(t + 1) * P], wb_s[:, l, 2048:2560])])
                                if tt == 0:
                                    sum_squares(c, B_QK - 1)
                        for c in range(CHUNKS):
                            pe.wait_ge(rsp_rdy, l * CHUNKS + c + 1)
                            for tt in range(TPC):
                                mm = pe.transpose(bank[0:48, 6 + c, tt * 64:(tt + 1) * 64].bitcast(BF16),
                                                  rsp[:, c, tt, :], identb)
                            mm.then_inc(rt_full, 1)
                        for c in range(CHUNKS):
                            pe.wait_ge(rt_rdy, l * CHUNKS + c + 1)
                            for k in range(B_QK):
                                product(USE0[f"norm{l}"] + c * 8 + k, [(seln[:, k * P:(k + 1) * P], rT[:, c, :])])
                        attention(l)
                        for c in range(CHUNKS):
                            pe.wait_ge(ot_rdy, ot_n(l, (c + 1) * TPC))
                            product(USE0[f"wo{l}"] + c, [(wob_s[:, l, f, :], oT[:, f, cc(c)]) for f in range(4)])
                        layernorm(f"ln{l}", lambda c: hT[:, cc(c)],
                                  lambda c: pe.wait_ge(shift_rdy, l * 4 + 2 + c + 1))
                        u = USE0[f"ffn{l}"]
                        for c in range(CHUNKS):
                            pe.wait_ge(hn_rdy, (l + 1) * CHUNKS + c + 1)
                            for f, (s, w) in enumerate(HID_T):
                                product(u + c * 7 + 2 * f, [(w1_s[:, l, s:s + w], hT[:, cc(c)])])
                                product(u + c * 7 + 2 * f + 1, [(w1_s[:, l, HID + s:HID + s + w], hT[:, cc(c)])])
                            for f in range(3):
                                taken(pe, u + c * 7 + 2 * f)
                            product(u + c * 7 + 6, [(w2_s[0:w, l, f, :], oT[0:w, f, cc(c)])
                                                    for f, (s, w) in enumerate(HID_T)])
                    for c in range(CHUNKS):
                        i = USE0["out"] + c
                        pe.wait_ge(fin_rdy, c + 1)
                        use_wait(pe, i)
                        for tt in range(TPC):
                            t = c * TPC + tt
                            mm = pe.transpose(bank[:, i % RING, tt * P:(tt + 1) * P], aT[:, t * P:(t + 1) * P],
                                              ident_s[:, :])
                        mm.then_inc(mm_full, 1)

                @block.scalar
                def _(act):
                    def attention(br):
                        A = br < 0
                        win = A_WIN if A else B_WIN
                        scale = A_HD ** -0.5 if A else 8.0

                        def copy_max(n):
                            act.wait_ge(mt_full, n + 1)
                            if n >= 2:
                                act.wait_ge(st_full, n - 1)
                            act.activation(mT[0:8, n % 2, :], x_bank[0:8, 0:64].bitcast(BF16), ACT.Copy)\
                               .then_inc(mt_rdy, 1)

                        def copy_heads(n):
                            _, t, _ = unit(n)
                            act.wait_ge(ot_full, ot_n(br, t) + 1)
                            F = 1 if A else 4
                            act.activation(oT[:, 0:F, t * P:(t + 1) * P],
                                           x_bank[:, 0:F * P].rearrange("p (f q) -> p f q", f=F), ACT.Copy)\
                               .then_inc(ot_rdy, 1)

                        last_g = A_KV - 1 if A else 1
                        for n in range(FIRST_UNIT[br], LAST_UNIT[br] + 1):
                            _, t, g = unit(n)
                            copy_max(n)
                            if g == 0 and t:
                                copy_heads(n - 1)
                            act.wait_ge(st_full, n + 1)
                            if n >= 2:
                                act.wait_ge(pv_done, n - 1)
                            e = slice(P - win, P)
                            if t:
                                act.activation(pcor[e, n % 2, 0:4 * win], c_bank[e, 0:4 * win], ACT.Exp, scale=scale)
                            act.activation(pm[:, n % 2, :], t_bank, ACT.Exp, scale=scale).then_inc(exp_done, 1)
                        copy_heads(LAST_UNIT[br])

                    def layernorm(name):
                        u = USE0[name]
                        for c in range(CHUNKS):
                            act.wait_ge(mm_full, u + c + 1)
                            act.activation(raw[:, c, :], bank[:, (u + c) % RING, :], ACT.Copy).then_inc(raw_rdy, 1)
                            act.activation(sq[:, c, :], bank[:, (u + c) % RING, :], ACT.Square)\
                               .then_inc(drained[(u + c) % RING], 1)
                        for c in range(CHUNKS):
                            i = u + CHUNKS + c
                            act.wait_ge(mm_full, i + 1)
                            act.activation(pc[:, c, :], bank[:, i % RING, :], ACT.Ln, bias=eps_s[:, 0:1])\
                               .then_inc(drained[i % RING], 1)
                            taken(act, i)
                            act.activation(ps_[:, c, :], pc[:, c, :], ACT.Exp, scale=-0.5).then_inc(rstd_rdy, 1)

                    for c in range(CHUNKS):
                        for w in range(2):
                            i = USE0["in"] + 2 * c + w
                            act.wait_ge(mm_full, i + 1)
                            act.activation(xc(c) if w == 0 else hT[:, cc(c)], bank[:, i % RING, :], ACT.Copy)\
                               .then_inc(drained[i % RING], 1)
                    i = USE0["a_proj"] + 20
                    act.wait_ge(mm_full, i + 1)
                    act.activation(vA[:, :, :, 0:A_HD],
                                   bank[:, i % RING, 0:256].rearrange("p (t g d) -> p t g d", t=TILES, g=A_KV),
                                   ACT.Copy).then_inc(drained[i % RING], 1)
                    attention(-1)
                    layernorm("a_ln")
                    u = USE0["a_ffn"]
                    for c in range(CHUNKS):
                        for f in range(4):
                            i = u + c * 5 + f
                            act.wait_ge(mm_full, i + 1)
                            act.activation(oT[:, f, cc(c)], bank[:, i % RING, :], ACT.Gelu,
                                           bias=bias[:, V_BF1 + f:V_BF1 + f + 1]).then_inc(drained[i % RING], 1)
                    for l in range(LAYERS):
                        u = USE0[f"proj{l}"]
                        for c in range(CHUNKS):
                            for k in range(B_QK):
                                i, j = u + c * 20 + 2 * k, pair(l, c, k)
                                jb = j - 10
                                act.wait_ge(mm_full, i + 1)
                                if jb >= 2:
                                    act.wait_ge(prod_rdy, jb - 1)
                                act.activation(raw[:, j % 2, :], bank[:, i % RING, :], ACT.Copy).then_inc(raw_rdy, 1)
                                if jb >= 2:
                                    act.wait_ge(ss_done, jb - 1)
                                act.activation(sq[:, j % 2, :], bank[:, i % RING, :], ACT.Square)\
                                   .then_inc(drained[i % RING], 1)
                            for tt in range(TPC):
                                i, t = u + c * 20 + 16 + tt, c * TPC + tt
                                act.wait_ge(mm_full, i + 1)
                                act.wait_ge(pv_done, FIRST_UNIT[l])
                                act.activation(vB[:, t, :, 0:B_HD],
                                               bank[:, i % RING, :].rearrange("p (h d) -> p h d", h=B_H), ACT.Copy)\
                                   .then_inc(drained[i % RING], 1)
                        for c in range(CHUNKS):
                            act.wait_ge(rt_full, l * CHUNKS + c + 1)
                            act.activation(rT[:, c, :], bank[0:48, 6 + c, 0:256].bitcast(BF16), ACT.Copy)\
                               .then_inc(rt_rdy, 1)
                        attention(l)
                        layernorm(f"ln{l}")
                        u = USE0[f"ffn{l}"]
                        for c in range(CHUNKS):
                            for f, (s, w) in enumerate(HID_T):
                                i = u + c * 7 + 2 * f + 1
                                n = (l * CHUNKS + c) * 3 + f
                                act.wait_ge(mm_full, i + 1)
                                if f == 2:
                                    taken(act, i - 5)
                                elif c:
                                    taken(act, i - 6)
                                bc = V_L + l * VL_N + VL_B1 + 3 + f
                                act.activation(gel[0:w, n % 2, :], bank[0:w, i % RING, :], ACT.Gelu,
                                               bias=bias[0:w, bc:bc + 1]).then_inc(drained[i % RING], 1)

                @block.vector
                def _(dve):
                    steps = [0]

                    def link(ins):
                        steps[0] += 1
                        ins.then_inc(v_link, 1)
                        dve.wait_ge(v_link, steps[0])

                    def token_norm(t, src, dst):
                        link(dve.bn_stats(stat[:, 0:6], src[:, t, :]))
                        link(dve.bn_aggr(mv[:, 0:2], stat[:, 0:6]))
                        inv_root(mv[:, 1:2], EPS, ALU.add, 1)
                        dve.tensor_scalar(dst[:, t, :], src[:, t, :], mv[:, 0:1], nw[:, 1, 0:1], ALU.subtract,
                                          ALU.mult).then_inc(tok_norm, 1)

                    def inv_root(src, c, op, n):
                        v, y, t, s = (nw[:, r, 0:n] for r in range(4))
                        link(dve.tensor_scalar(v, src, c, None, op))
                        link(dve.tensor_scalar(y.bitcast(I32), v.bitcast(I32), -0.5, float(0x5F3759DF), ALU.mult,
                                               ALU.add))
                        for _ in range(4):
                            link(dve.tensor_tensor(t, y, y, ALU.mult))
                            link(dve.scalar_tensor_tensor(s, t, -0.5, v, ALU.mult, ALU.mult))
                            link(dve.scalar_tensor_tensor(y, s, 1.5, y, ALU.add, ALU.mult))

                    def rotate(br, c, k, i, ct, st):
                        j = pair(br, c, k)
                        A = br < 0
                        if j >= 2:
                            dve.wait_ge(sum_rdy, j - 1)
                        if A:
                            bq, bqr = (V_BQ + k, V_BQR + k) if k < 4 else (V_BK, V_BKR)
                            dve.wait_ge(mm_full, i + 1)
                            dve.scalar_tensor_tensor(pc[:, j % 2, :], bank[:, i % RING, :], bias[:, bq:bq + 1], ct,
                                                     ALU.add, ALU.mult).then_inc(drained[i % RING], 1)
                            dve.wait_ge(mm_full, i + 2)
                            dve.scalar_tensor_tensor(ps_[:, j % 2, :], bank[:, (i + 1) % RING, :],
                                                     bias[:, bqr:bqr + 1], st, ALU.add, ALU.mult)\
                               .then_inc(drained[(i + 1) % RING], 1)
                        else:
                            raws = RAW0[br] + c * 8 + k
                            dve.wait_ge(mm_full, i + 2)
                            dve.tensor_tensor(ps_[:, j % 2, :], bank[:, (i + 1) % RING, :], st, ALU.mult)\
                               .then_inc(drained[(i + 1) % RING], 1)
                            dve.wait_ge(raw_rdy, raws + 1)
                            dve.tensor_tensor(pc[:, j % 2, :], raw[:, j % 2, :], ct, ALU.mult).then_inc(prod_rdy, 1)

                    RAW0 = {0: 2, 1: 2 + 16 + 2}
                    RAWLN = {"a_ln": 0, "ln0": 2 + 16, "ln1": 2 + 16 + 2 + 16}

                    def attention(br):
                        A = br < 0
                        hd, win = (A_HD, A_WIN) if A else (B_HD, B_WIN)

                        def maxima(n):
                            _, t, _ = unit(n)
                            w = P if t == 0 else P + win
                            dve.wait_ge(sc_full, n + 1)
                            if n >= 2:
                                dve.wait_ge(mt_full, n - 1)
                            link(dve.tensor_reduce(mx[:, n % 2, :],
                                                   s_bank[n % 2][:, :, 0:2 * w].rearrange("p b (h w) -> p b h w", h=2),
                                                   AX_X, ALU.max))
                            link(dve.tensor_scalar(negm[:, n % 2, 0:4], mx[:, n % 2, :], -1.0, None, ALU.mult))
                            dve.scalar_tensor_tensor(negm[:, n % 2, 4:8], mx[:, n % 2, :], -1.0, negm[:, n % 2, 0:4],
                                                     ALU.mult, ALU.subtract).then_inc(max_rdy, 1)

                        def normalise(n):
                            _, t, g = unit(n)
                            o = o_bank[:, 0:4 * (hd + 1)].rearrange("p (h d) -> p h d", h=4)
                            dve.wait_ge(pv_done, n + 1)
                            per = ot_n(br, t)
                            if t >= 2:
                                dve.wait_ge(ot_full, per - 1)
                            link(dve.reciprocal(rl[:, :], o[:, :, hd]))
                            if A:
                                dst = o_tok[:, t % 2, g * 4 * hd:(g + 1) * 4 * hd].rearrange("p (h d) -> p h d", h=4)
                            else:
                                dst = o_tok[:, t % 2, :].rearrange("p (h g d) -> p h g d", h=4, g=2)[:, :, g, :]
                            dve.tensor_tensor(dst, o[:, :, 0:hd], rl[:, :].unsqueeze(2).to_broadcast([P, 4, hd]),
                                              ALU.mult).then_inc(on_rdy, 1)

                        maxima(FIRST_UNIT[br])
                        for n in range(FIRST_UNIT[br], LAST_UNIT[br] + 1):
                            if n < LAST_UNIT[br]:
                                maxima(n + 1)
                            if n > FIRST_UNIT[br]:
                                normalise(n - 1)
                        normalise(LAST_UNIT[br])

                    def layernorm(name):
                        for c in range(CHUNKS):
                            dve.wait_ge(raw_rdy, RAWLN[name] + c + 1)
                            dve.wait_ge(rstd_rdy, ln_n(name, c) + 1)
                            dve.tensor_tensor(hT[:, cc(c)], raw[:, c, :], ps_[:, c, :], ALU.mult).then_inc(hn_rdy, 1)

                    def shift():
                        for c in range(CHUNKS):
                            dve.tensor_copy(hT[0:64, cc(c)], xT[0:64, 1 + c * CH:1 + (c + 1) * CH])
                            dve.tensor_copy(hT[64:128, cc(c)], xT[64:128, c * CH:(c + 1) * CH])\
                               .then_inc(shift_rdy, 1)

                    dve.wait_ge(x_in, 16)
                    for t in range(TILES):
                        token_norm(t, x_tok, rt_tok)
                    for t in range(TILES):
                        dve.wait_ge(tok_norm, t + 1)
                        token_norm(t, rt_tok, h_tok)
                    u = USE0["a_proj"]
                    for c in range(CHUNKS):
                        for k in range(5):
                            rotate(-1, c, k, u + c * 10 + 2 * k, tab_s[:, 4, cc(c)], tab_s[:, 5, cc(c)])
                    attention(-1)
                    for c in range(CHUNKS):
                        i = USE0["a_wo"] + c
                        dve.wait_ge(mm_full, i + 1)
                        dve.scalar_tensor_tensor(aT[:, cc(c)], bank[:, i % RING, :], bias[:, V_BO:V_BO + 1], xc(c),
                                                 ALU.add, ALU.add).then_inc(drained[i % RING], 1)
                    layernorm("a_ln")
                    for c in range(CHUNKS):
                        i = USE0["a_ffn"] + c * 5 + 4
                        dve.wait_ge(mm_full, i + 1)
                        dve.scalar_tensor_tensor(aT[:, cc(c)], bank[:, i % RING, :], vec_s[:, V_BF2:V_BF2 + 1],
                                                 aT[:, cc(c)], ALU.add, ALU.add).then_inc(drained[i % RING], 1)
                    for l in range(LAYERS):
                        vl = V_L + l * VL_N
                        shift()
                        for r, (tab, g) in enumerate(((0, 0), (1, 1), (2, 2), (3, 3))):
                            dve.tensor_scalar(rt_tab[:, r, :], tab_s[:, tab, :], vec_s[:, vl + VL_QS + g:vl + VL_QS + g + 1],
                                              None, ALU.mult).then_inc(v_link, 1)
                            steps[0] += 1
                        dve.wait_ge(v_link, steps[0])
                        u = USE0[f"proj{l}"]
                        for c in range(CHUNKS):
                            for k in range(B_QK):
                                r = 0 if k < 4 else 2
                                rotate(l, c, k, u + c * 20 + 2 * k, rt_tab[:, r, cc(c)], rt_tab[:, r + 1, cc(c)])
                        for c in range(CHUNKS):
                            dve.wait_ge(ss_done, (l * CHUNKS + c + 1) * B_QK)
                            inv_root(bank[:, 4 + c, 0:64], 1e-24, ALU.max, 64)
                            y, r_ = nw[:, 1, :], nw[:, 2, :]
                            part = [rsp[:, c, :, 16 * m:16 * (m + 1)] for m in range(3)]
                            y, r_ = (z.rearrange("p (t k) -> p t k", t=TPC) for z in (y, r_))
                            link(dve.tensor_copy(part[0], y))
                            link(dve.tensor_tensor(r_, y, part[0], ALU.subtract))
                            link(dve.tensor_copy(part[1], r_))
                            dve.tensor_tensor(part[2], r_, part[1], ALU.subtract).then_inc(rsp_rdy, 1)
                        for c in range(CHUNKS):
                            for k in range(B_QK):
                                i = USE0[f"norm{l}"] + c * 8 + k
                                dve.wait_ge(sum_rdy, pair(l, c, k) + 1)
                                dve.wait_ge(mm_full, i + 1)
                                dve.tensor_tensor(qk[:, k, cc(c)], bank[:, i % RING, :], qk[:, k, cc(c)], ALU.mult)\
                                   .then_inc(drained[i % RING], 1)
                        attention(l)
                        for c in range(CHUNKS):
                            i = USE0[f"wo{l}"] + c
                            dve.wait_ge(mm_full, i + 1)
                            dve.tensor_tensor(xc(c), bank[:, i % RING, :], xc(c), ALU.add)\
                               .then_inc(drained[i % RING], 1)
                            taken(dve, i)
                        shift()
                        layernorm(f"ln{l}")
                        u = USE0[f"ffn{l}"]
                        for c in range(CHUNKS):
                            for f, (s, w) in enumerate(HID_T):
                                i = u + c * 7 + 2 * f
                                n = (l * CHUNKS + c) * 3 + f
                                dve.wait_ge(mm_full, i + 1)
                                taken(dve, i + 1)
                                bc = vl + VL_B1 + f
                                dve.scalar_tensor_tensor(oT[0:w, f, cc(c)], bank[0:w, i % RING, :],
                                                         bias[0:w, bc:bc + 1], gel[0:w, n % 2, :], ALU.add,
                                                         ALU.mult).then_inc(drained[i % RING], 1)
                            i = u + c * 7 + 6
                            dve.wait_ge(mm_full, i + 1)
                            dve.scalar_tensor_tensor(xc(c), bank[:, i % RING, :],
                                                     vec_s[:, vl + VL_B2:vl + VL_B2 + 1], xc(c), ALU.add,
                                                     ALU.add).then_inc(drained[i % RING], 1)
                            taken(dve, i)
                    for c in range(CHUNKS):
                        dve.tensor_tensor(aT[:, cc(c)], aT[:, cc(c)], xc(c), ALU.add).then_inc(fin_rdy, 1)
                    for c in range(CHUNKS):
                        i = USE0["out"] + c
                        dve.wait_ge(mm_full, i + 1)
                        tt = slice(c * TPC, (c + 1) * TPC)
                        dve.tensor_tensor(x_tok[:, tt, :], bank[:, i % RING, :].rearrange("p (t d) -> p t d", d=D),
                                          x_tok[:, tt, :], ALU.add).then_inc(out_rdy, 1)

            nc.all_engine_barrier(sems_to_clear=range(first, last + 1))


def host_constants():
    import numpy as np
    f = np.float32
    pos = np.arange(T, dtype=f)
    half = np.arange(0, B_HD, 2, dtype=f)
    inv = (f(1.0) / np.power(f(10000.0), half / f(B_HD))).astype(f)
    fr = (pos[:, None] * inv[None, :]).astype(f)
    fr = np.concatenate([fr, fr], axis=-1)
    base = ((half + f(0.4 * B_HD)) / f(1.4 * B_HD)).astype(f)
    power = ((pos - f(T // 2)) / f(B_WIN // 2)).astype(f)
    sc = np.power(base[None, :], power[:, None]).astype(f)
    sc = np.concatenate([sc, sc], axis=-1)
    sign = np.where(np.arange(B_HD) < B_HD // 2, f(-1), f(1))
    cos, sin = np.cos(fr).astype(f), np.sin(fr).astype(f) * sign
    tabs = np.zeros((P, 6, T), f)
    for r, tab in enumerate((cos * sc, sin * sc, cos / sc, sin / sc)):
        tabs[:, r, :] = np.concatenate([tab, tab], axis=1).T
    th = (f(1.0) / np.power(f(10000.0), np.arange(A_HD // 2, dtype=f) / f(A_HD // 2))).astype(f)
    fr = (pos[:, None] * th[None, :]).astype(f)
    for g in range(A_KV):
        for d in range(A_HD):
            a = fr[:, d % (A_HD // 2)]
            tabs[32 * g + d, 4] = np.cos(a)
            tabs[32 * g + d, 5] = np.sin(a) * (f(-1) if d < A_HD // 2 else f(1))
    ident = np.eye(P, dtype=f)
    center = (ident - f(1.0 / P)).astype(f)
    ones = np.zeros((P, P + 2), f)
    ones[:, :P] = 1.0 / P
    ones[:64, P] = 1
    ones[64:, P + 1] = 1
    r = np.arange(P)

    def allow(diff, win, strict):
        ok = (diff >= 0) & ((diff < win) if strict else (diff <= win))
        return np.where(ok, f(0), f(-1e30))

    parts = [ident]
    for win, s in ((A_WIN, True), (B_WIN, False)):
        parts.append(np.tile(allow(r[:, None] - (np.arange(P + win)[None, :] - win), win, s), (1, 2)))
    for win, s in ((A_WIN, True), (B_WIN, False)):
        parts.append(np.tile(allow(r[:, None] - r[None, :], win, s), (1, 2)))
    for win, s in ((A_WIN, True), (B_WIN, False)):
        parts.append(np.tile(allow(r[None, :] - r[:, None], win, s), (1, 4)))
    for win, s in ((A_WIN, True), (B_WIN, False)):
        parts.append(np.tile(allow(P + np.arange(win)[None, :] - r[:, None], win, s), (1, 4)))
    selm = np.zeros((P, 4, P), f)
    for h in range(4):
        selm[h, h] = 1
        selm[4 + h, h] = 1
    seln = np.zeros((P, B_QK, P), f)
    for k in range(B_QK):
        for m in range(3):
            seln[16 * m + 2 * k, k, :64] = 1
            seln[16 * m + 2 * k + 1, k, 64:] = 1
    parts += [selm.reshape(P, -1), seln.reshape(P, -1)]
    cbf = np.concatenate(parts, axis=1).astype(np.dtype("bfloat16"))
    return dict(tabs=tabs, ident=ident, center=center, ones=ones, cbf=cbf)


def host_layout(i):
    import numpy as np
    f = np.float32
    n = {k[3:]: np.asarray(v) for k, v in i.items()}
    wq, wk, wv = n["attn_Wq"], n["attn_Wk"], n["attn_Wv"]
    bq, bk, bv = n["attn_bq"], n["attn_bk"], n["attn_bv"]
    wa = np.zeros((P, WA_N), f)
    vec = np.zeros((P, V_N), f)
    turn = (np.arange(A_HD) + A_HD // 2) % A_HD
    for g in range(A_KV):
        rows = slice(32 * g, 32 * g + A_HD)
        for j in range(A_GRP):
            h = A_GRP * g + j
            cols = A_HD * h + np.arange(A_HD)
            for off, voff, cl in ((WA_Q, V_BQ, cols), (WA_QR, V_BQR, A_HD * h + turn)):
                wa[:, off + j * P + 32 * g:off + j * P + 32 * g + A_HD] = wq[:, cl]
                vec[rows, voff + j] = bq[cl]
        for off, voff, cl in ((WA_K, V_BK, A_HD * g + np.arange(A_HD)), (WA_KR, V_BKR, A_HD * g + turn)):
            wa[:, off + 32 * g:off + 32 * g + A_HD] = wk[:, cl]
            vec[rows, voff] = bk[cl]
    wa[:, WA_V:] = wv
    rep = np.concatenate([A_HD * (h // A_GRP) + np.arange(A_HD) for h in range(16)])
    wvr = np.ascontiguousarray(wv[:, rep])
    vec[:, V_BVR] = bv[rep]
    for c, k in ((V_G1, "attn_g1"), (V_B1, "attn_b1"), (V_G2, "attn_g2"), (V_B2, "attn_b2"), (V_BO, "attn_bo"),
                 (V_BF2, "attn_bf2")):
        vec[:, c] = n[k]
    vec[:, V_BF1:V_BF1 + 4] = n["attn_bf1"].reshape(4, P).T
    wf2 = np.ascontiguousarray(n["attn_Wf2"].reshape(4, P, D).transpose(1, 0, 2))
    wqkv = n["ffn_wqkv"]
    turn = (np.arange(B_HD) + B_HD // 2) % B_HD
    cols = np.concatenate([B_HD * h + turn for h in range(2 * B_H)])
    wb = np.ascontiguousarray(np.concatenate([wqkv[:, :, :1024], wqkv[:, :, cols], wqkv[:, :, 1024:]], axis=2)
                              .transpose(1, 0, 2))
    wob = np.ascontiguousarray(n["ffn_wo"].reshape(LAYERS, 4, P, D).transpose(2, 0, 1, 3))
    w1 = np.ascontiguousarray(n["ffn_w1"].transpose(1, 0, 2))
    w2 = np.zeros((P, LAYERS, 3, P), f)
    for l in range(LAYERS):
        o = V_L + l * VL_N
        vec[:, o + VL_G], vec[:, o + VL_B], vec[:, o + VL_B2] = n["ffn_ln_g"][l], n["ffn_ln_b"][l], n["ffn_b2"][l]
        for q, (k, t) in enumerate((("q", 0), ("q", 1), ("k", 0), ("k", 1))):
            s = n[f"ffn_{k}_scale"][l]
            vec[:, o + VL_QS + q] = np.concatenate([s[turn] if t else s] * 2)
        for hf in range(2):
            for t, (s, w) in enumerate(HID_T):
                vec[:w, o + VL_B1 + 3 * hf + t] = n["ffn_b1"][l, hf * HID + s:hf * HID + s + w]
        for t, (s, w) in enumerate(HID_T):
            w2[:w, l, t] = n["ffn_w2"][l, s:s + w]
    return dict(x=n["attn_x"], wa=wa, wo=n["attn_Wo"], wf1=n["attn_Wf1"], wf2=wf2, wvr=wvr, vec=vec, wb=wb,
                wob=wob, w1=w1, w2=w2)


def kernel(**inputs):
    import numpy as np
    import concourse.bacc as bacc
    from concourse.bass_utils import run_bass_kernel_spmd

    nc = bacc.Bacc("TRN2", target_bir_lowering=False, num_devices=1)
    arrays = {k: np.ascontiguousarray(v) for k, v in {**host_layout(inputs), **host_constants()}.items()}
    args = {k: nc.dram_tensor(k, v.shape, mybir.dt.from_np(v.dtype), kind="ExternalInput").ap()
            for k, v in arrays.items()}
    out = nc.dram_tensor("out", (BATCH, T, D), F32, kind="ExternalOutput").ap()
    program(nc, out=out, **args)
    return run_bass_kernel_spmd(nc, [arrays], core_ids=[0]).results[0]["out"]
```

```python
from contextlib import ExitStack

import concourse.bass as bass
from concourse import mybir

F32 = mybir.dt.float32
F32R = mybir.dt.float32r
BF16 = mybir.dt.bfloat16
I32 = mybir.dt.int32
ALU = mybir.AluOpType
ACT = mybir.ActivationFunctionType
AX_X = mybir.AxisListType.X

P = 128
BATCH, T, D = 4, 1024, 128
TILES = T // P
CH = 512
CHUNKS = T // CH
TPC = CH // P
LAYERS = 2
A_KV, A_GRP, A_HD, A_WIN, A_FF = 4, 4, 8, 32, 4
B_H, B_HD, B_WIN = 8, 64, 64
B_QK = 2 * B_H * B_HD // P
HID = 341
HID_T = [(0, 128), (128, 128), (256, HID - 256)]
EPS = 1e-5

A_UNITS = TILES * A_KV
B_UNITS = TILES * B_H // 4
UNITS = A_UNITS + LAYERS * B_UNITS

WA_Q, WA_QR, WA_K, WA_KR, WA_V = 0, 512, 1024, 1152, 1280
WA_N = 1312
(V_G1, V_B1, V_G2, V_B2, V_BO, V_BF2, V_BVR, V_BQ, V_BQR, V_BK, V_BKR, V_BF1, V_SQ, V_SK) = (
    0, 1, 2, 3, 4, 5, 6, 7, 11, 15, 16, 17, 21, 22)
V_L = 23
(VL_G, VL_B, VL_B2, VL_QS, VL_B1) = (0, 1, 2, 3, 7)
VL_N = 13
V_N = V_L + LAYERS * VL_N

STAGES = [("in", 4), ("a_proj", 21), ("a_norm", 8), ("a_wo", 2), ("a_ln", 4), ("a_ffn", 10)]
for _l in range(LAYERS):
    STAGES += [(f"proj{_l}", 40), (f"norm{_l}", 16), (f"wo{_l}", 2), (f"ln{_l}", 4), (f"ffn{_l}", 14)]
STAGES += [("out", 2)]
USE0 = {}
_n = 0
for _name, _k in STAGES:
    USE0[_name] = _n
    _n += _k
RING = 4


def unit(n):
    if n < A_UNITS:
        return -1, n // A_KV, n % A_KV
    m = n - A_UNITS
    return m // B_UNITS, m % B_UNITS // 2, m % 2


def program(nc, x, wa, wo, wf1, wf2, wvr, vec, wb, wob, w1, w2, tabs, ident, center, ones, pick, cbf, out):
    ctx = ExitStack()
    with ctx:
        def sb(name, shape, dt=F32):
            return ctx.enter_context(nc.sbuf_tensor(name, shape, dt))

        def sem(name):
            return ctx.enter_context(nc.semaphore(name))

        wa_s = sb("wa_s", [P, WA_N])
        wo_s = sb("wo_s", [P, A_GRP, D])
        wf1_s = sb("wf1_s", [P, A_FF * P])
        wf2_s = sb("wf2_s", [P, A_FF, P])
        vec_s = sb("vec_s", [P, V_N])
        bias = sb("bias", [P, V_N])
        wb_s = sb("wb_s", [P, LAYERS, 2560])
        wob_s = sb("wob_s", [P, LAYERS, 4, P])
        w1_s = sb("w1_s", [P, LAYERS, 2 * HID])
        w2_s = sb("w2_s", [P, LAYERS, 3, P])
        tab_s = sb("tab_s", [P, 6, T])
        ident_s = sb("ident_s", [P, P])
        center_s = sb("center_s", [P, P])
        ones_s = sb("ones_s", [P, P + 2])
        pick_s = sb("pick_s", [P, P])
        eps_s = sb("eps_s", [P, 1])
        CB = cbf.shape[1]
        cbf_s = sb("cbf_s", [P, CB], BF16)
        o = 0
        identb = cbf_s[:, 0:128]
        o = 128
        smask = {-1: cbf_s[:, o:o + 320], 0: cbf_s[:, o + 320:o + 704]}
        o += 704
        smask0 = {-1: cbf_s[:, o:o + 256], 0: cbf_s[:, o + 256:o + 512]}
        o += 512
        tmask = {-1: cbf_s[:, o:o + 512], 0: cbf_s[:, o + 512:o + 1024]}
        o += 1024
        cmask = {-1: cbf_s[:, o:o + 128], 0: cbf_s[:, o + 128:o + 384]}
        o += 384
        selm = cbf_s[:, o:o + 512]
        o += 512
        seln = cbf_s[0:48, o:o + 1024]
        o += 1024
        assert o == CB

        x_tok = sb("x_tok", [P, TILES, D])
        xT = sb("xT", [P, T + 1])
        aT = sb("aT", [P, T])
        hT = sb("hT", [P, T])
        with nc.sbuf_tensor("qA", [P, A_GRP, T], F32R) as qA, nc.sbuf_tensor("kA", [P, A_KV, T], F32R) as kA:
            pass
        qk = sb("qk", [P, B_QK, T])
        vB = sb("vB", [P, TILES, 4, 3 * B_HD])
        vA = sb("vA", [P, TILES, A_KV, 32])
        oT = sb("oT", [P, 4, T])
        with nc.sbuf_tensor("rec", [P, A_GRP, T], F32) as rec:
            pass
        raw = sb("raw", [P, 2, CH])
        with nc.sbuf_tensor("hiA", [P, 2, CH], F32R) as hiA:
            pass
        sq = sb("sq", [P, 2, CH])
        pc = sb("pc", [P, 2, CH])
        ps_ = sb("ps_", [P, 2, CH])
        pm = sb("pm", [P, 2, 512])
        pcor = sb("pcor", [P, 2, 256])
        gel = pm
        stat = sb("stat", [P, TILES, 6])
        mv = sb("mv", [P, TILES, 2])
        nw = sb("nw", [P, 4, 64])
        rsp = sb("rsp", [P, 2, TPC, 48], BF16)
        rT = sb("rT", [48, 2, CH], BF16)
        mx = sb("mx", [P, 2, 4])
        negm = sb("negm", [P, 2, 8], BF16)
        mT = sb("mT", [P, 2, P], BF16)
        sums = sb("sums", [P, 2, 512])
        rl = sb("rl", [P, 512])

        bank = ctx.enter_context(nc.psum_tensor("bank", [P, 8, 512], F32))
        s_bank = [bank[:, 0:2, :], bank[:, 2:4, :]]
        t_bank, c_bank, o_bank, x_bank = (bank[:, b, :] for b in (4, 5, 6, 7))

        s_load = sem("weights_loaded")
        setup_v = sem("setup_vector")
        setup_p = sem("setup_pool")
        setup_mm = sem("setup_products")
        first = s_load.num
        x_in = sem("x_loaded")
        tok_norm = sem("tokens_normed")
        mm_full = sem("product_ready")
        drained = [sem(f"bank{b}_drained") for b in range(RING)]
        raw_rdy = sem("raw_copied")
        prod_rdy = sem("rotary_products")
        sum_rdy = sem("rotated")
        ss_done = sem("squares_summed")
        rsp_rdy = sem("norms_split")
        rt_full = sem("norms_turned")
        rt_rdy = sem("norms_copied")
        shift_rdy = sem("shifted")
        sc_full = sem("scores_ready")
        max_rdy = sem("maxima_ready")
        mt_full = sem("maxima_turned")
        mt_rdy = sem("maxima_copied")
        st_full = sem("key_scores_ready")
        exp_done = sem("probs_ready")
        pv_done = sem("values_weighted")
        on_rdy = sem("heads_normalised")
        hi_rdy = sem("leading_halves")
        split_rdy = sem("halves_laid_out")
        kz_rdy = sem("keys_zeroed")
        rec_rdy = sem("sums_inverted")
        ob_rdy = sem("heads_and_sums_copied")
        ot_rdy = sem("heads_copied")
        rstd_rdy = sem("rstd_ready")
        hn_rdy = sem("ln_ready")
        fin_rdy = sem("branches_added")
        out_rdy = sem("out_ready")
        out_done = sem("out_stored")
        v_link = sem("vector_step")
        last = v_link.num

        def xc(c):
            return xT[:, 1 + c * CH:1 + (c + 1) * CH]

        def cc(c):
            return slice(c * CH, (c + 1) * CH)

        biases = [(wa_s[:, WA_Q + j * P:WA_Q + (j + 1) * P], V_B1, V_BQ + j) for j in range(4)]
        biases += [(wa_s[:, WA_QR + j * P:WA_QR + (j + 1) * P], V_B1, V_BQR + j) for j in range(4)]
        biases += [(wa_s[:, WA_K:WA_K + P], V_B1, V_BK), (wa_s[:, WA_KR:WA_KR + P], V_B1, V_BKR)]
        biases += [(wf1_s[:, f * P:(f + 1) * P], V_B2, V_BF1 + f) for f in range(4)]
        for l in range(LAYERS):
            for half in range(2):
                for f, (s, w) in enumerate(HID_T):
                    biases.append((w1_s[:, l, half * HID + s:half * HID + s + w], V_L + l * VL_N + VL_B,
                                   V_L + l * VL_N + VL_B1 + half * 3 + f))
        NB = len(biases)
        wvr_s = aT[:, 0:P]

        with nc.Block() as block:
            @block.sync
            def _(sp):
                for dst, src in ((wa_s[:, :], wa), (vec_s[:, :], vec), (wo_s[:, :, :], wo), (wf1_s[:, :], wf1),
                                 (wf2_s[:, :, :], wf2), (wvr_s, wvr), (w1_s[:, :, :], w1),
                                 (wb_s[:, :, :], wb), (tab_s[:, :, :], tabs)):
                    sp.dma_start(dst, src).then_inc(s_load, 16)

            @block.scalar
            def _(act):
                for dst, src in ((ident_s[:, :], ident), (center_s[:, :], center), (ones_s[:, :], ones), (pick_s[:, :], pick),
                                 (cbf_s[:, :], cbf), (wob_s[:, :, :, :], wob), (w2_s[:, :, :, :], w2)):
                    act.dma_start(dst, src).then_inc(s_load, 16)

            @block.gpsimd
            def _(pool):
                pool.memset(vB[:, :, :, B_HD:2 * B_HD], 1.0).then_inc(setup_p, 1)
                pool.memset(vA[:, :, :, A_HD:32], 1.0).then_inc(setup_p, 1)
                pool.memset(xT[:, 0:1], 0.0).then_inc(setup_p, 1)
                pool.memset(eps_s[:, :], EPS).then_inc(setup_p, 1)
                pool.memset(mT[:, :, :], 0.0).then_inc(setup_p, 1)

            @block.tensor
            def _(pe):
                pe.wait_ge(s_load, 16 * 16)
                for n, (w, b, _) in enumerate(biases):
                    pe.matmul(bank[0:w.shape[1], 0, n:n + 1], w, vec_s[:, b:b + 1], start=True, stop=True)
                pe.matmul(bank[:, 0, NB:NB + 1], wvr_s, vec_s[:, V_B1:V_B1 + 1],
                          start=True, stop=True).then_inc(setup_mm, 1)
                pe.wait_ge(setup_v, 1)
                for j in range(A_GRP):
                    mm = pe.matmul(bank[:, 1, 0:1], wo_s[:, j, :], bias[:, V_BVR:V_BVR + 1],
                                   start=(j == 0), stop=(j == A_GRP - 1))
                mm.then_inc(setup_mm, 1)

            @block.vector
            def _(dve):
                dve.wait_ge(s_load, 16 * 16)
                dve.wait_ge(setup_mm, 1)
                dve.tensor_tensor(bias[:, V_BVR:V_BVR + 1], bank[:, 0, NB:NB + 1], vec_s[:, V_BVR:V_BVR + 1],
                                  ALU.add).then_inc(setup_v, 1)
                for n, (w, _, dst) in enumerate(biases):
                    m = w.shape[1]
                    dve.tensor_tensor(bias[0:m, dst:dst + 1], bank[0:m, 0, n:n + 1], vec_s[0:m, dst:dst + 1],
                                      ALU.add).then_inc(setup_v, 1)
                dve.tensor_scalar(wa_s[:, :], wa_s[:, :], vec_s[:, V_G1:V_G1 + 1], None, ALU.mult).then_inc(setup_v, 1)
                dve.tensor_scalar(wf1_s[:, :], wf1_s[:, :], vec_s[:, V_G2:V_G2 + 1], None,
                                  ALU.mult).then_inc(setup_v, 1)
                for l in range(LAYERS):
                    g = V_L + l * VL_N + VL_G
                    dve.tensor_scalar(w1_s[:, l, :], w1_s[:, l, :], vec_s[:, g:g + 1], None,
                                      ALU.mult).then_inc(setup_v, 1)
                dve.wait_ge(setup_mm, 2)
                dve.tensor_tensor(bias[:, V_BO:V_BO + 1], bank[:, 1, 0:1], vec_s[:, V_BO:V_BO + 1],
                                  ALU.add).then_inc(setup_v, 1)

        def pair(br, c, k):
            return c * 5 + k if br < 0 else 10 + br * 16 + c * 8 + k

        def tile_of(n):
            return unit(n)[1]

        def taken(eng, i):
            eng.wait_ge(drained[i % RING], i // RING + 1)

        def use_wait(eng, i):
            if i >= RING:
                eng.wait_ge(drained[i % RING], i // RING)

        xn_tok, h_tok = (oT[:, r, :].rearrange("p (t d) -> p t d", d=D) for r in range(2))

        def ln_n(name, c):
            return {"a_ln": 0, "ln0": 1, "ln1": 2}[name] * CHUNKS + c

        def values_use(br, t):
            return USE0["a_proj"] + 20 if br < 0 else USE0[f"proj{br}"] + t // TPC * 20 + 16 + t % TPC

        LAST_UNIT = {-1: A_UNITS - 1, 0: A_UNITS + B_UNITS - 1, 1: UNITS - 1}
        FIRST_UNIT = {-1: 0, 0: A_UNITS, 1: A_UNITS + B_UNITS}

        with nc.Fori(0, BATCH) as b:
            with nc.Block() as block:
                x_b = x[bass.ds(b, 1), :, :].rearrange("a (t p) d -> p (a t) d", p=P)
                out_b = out[bass.ds(b, 1), :, :].rearrange("a (t p) d -> p (a t) d", p=P)

                @block.sync
                def _(sp):
                    sp.dma_start(x_tok[:, :, :], x_b).then_inc(x_in, 16)
                    for c in range(CHUNKS):
                        sp.wait_ge(out_rdy, c + 1)
                        sp.dma_start(out_b[:, c * TPC:(c + 1) * TPC, :],
                                     x_tok[:, c * TPC:(c + 1) * TPC, :]).then_inc(out_done, 16)
                    sp.wait_ge(out_done, 16 * CHUNKS)

                @block.gpsimd
                def _(pool):
                    pool.memset(kA[:, :, :].bitcast(F32), 0.0).then_inc(kz_rdy, 1)
                    for br in (-1, 0, 1):
                        for c in range(CHUNKS):
                            for k in range(5 if br < 0 else B_QK):
                                j = pair(br, c, k)
                                if br < 0:
                                    taken(pool, USE0["a_proj"] + c * 10 + 2 * k)
                                    taken(pool, USE0["a_proj"] + c * 10 + 2 * k + 1)
                                    if j >= 2:
                                        pool.wait_ge(split_rdy, j - 1)
                                    dst = raw[:, j % 2, :]
                                else:
                                    pool.wait_ge(prod_rdy, j - 10 + 1)
                                    taken(pool, USE0[f"proj{br}"] + c * 20 + 2 * k + 1)
                                    dst = qk[:, k, cc(c)]
                                if br >= 0 and c == 0 and k == 0:
                                    pool.wait_ge(st_full, FIRST_UNIT[br])
                                pool.tensor_tensor(dst, pc[:, j % 2, :], ps_[:, j % 2, :],
                                                   ALU.add).then_inc(sum_rdy, 1)

                @block.tensor
                def _(pe):
                    def product(i, parts, signal=True):
                        use_wait(pe, i)
                        m = parts[0][0].shape[1]
                        n = parts[0][1].shape[1]
                        for q, (lhs, rhs) in enumerate(parts):
                            mm = pe.matmul(bank[0:m, i % RING, 0:n], lhs, rhs, start=(q == 0),
                                           stop=(q == len(parts) - 1))
                        mm.then_inc(mm_full, 1)

                    def scores(n):
                        br, t, g = unit(n)
                        A = br < 0
                        w = P if t == 0 else P + (A_WIN if A else B_WIN)
                        if n - FIRST_UNIT[br] >= 2:
                            pe.wait_ge(max_rdy, n - 1)
                        elif n - FIRST_UNIT[br] == 0:
                            stop = USE0["a_norm"] if A else USE0[f"wo{br}"]
                            for i in range(stop - RING, stop):
                                taken(pe, i)
                        if A:
                            pe.wait_ge(split_rdy, pair(br, t // TPC, 4) + 1)
                        else:
                            for k in range(B_QK - RING, B_QK):
                                taken(pe, USE0[f"norm{br}"] + t // TPC * B_QK + k)
                        mask = (smask0 if t == 0 else smask)[min(br, 0)]
                        q0, k0 = t * P, (t + 1) * P - w
                        for h in range(4):
                            dst = s_bank[n % 2][:, h // 2, :]
                            if h % 2 == 0:
                                pe.matmul(dst[:, 0:2 * w], identb, mask, start=True, stop=False,
                                          skip_group_check=True)
                            if A:
                                mm = pe.matmul(dst[:, (h % 2) * w:(h % 2 + 1) * w], qA[:, h, q0:q0 + P],
                                               kA[:, g, k0:k0 + w], start=False, stop=(h % 2 == 1),
                                          skip_group_check=True)
                            else:
                                r = slice(64 * g, 64 * g + 64)
                                mm = pe.matmul(dst[:, (h % 2) * w:(h % 2 + 1) * w], qk[r, h, q0:q0 + P],
                                               qk[r, 4 + h, k0:k0 + w], start=False, stop=(h % 2 == 1),
                                               skip_group_check=True)
                        mm.then_inc(sc_full, 1)

                    def turn_max(n):
                        pe.wait_ge(max_rdy, n + 1)
                        if n >= 1:
                            pe.wait_ge(mt_rdy, n)
                        pe.transpose(x_bank[0:8, 0:64].bitcast(BF16), negm[:, n % 2, :], identb).then_inc(mt_full, 1)

                    def key_scores(n):
                        br, t, g = unit(n)
                        A = br < 0
                        win = A_WIN if A else B_WIN
                        pe.wait_ge(mt_rdy, n + 1)
                        if n >= 1:
                            pe.wait_ge(exp_done, n)
                        q0 = t * P
                        rows = slice(64 * g, 64 * g + 64)
                        pe.matmul(t_bank, identb, tmask[min(br, 0)], start=True, stop=False, skip_group_check=True)
                        for h in range(4):
                            pe.matmul(t_bank[:, h * P:(h + 1) * P], selm[:, h * P:(h + 1) * P], mT[:, n % 2, :],
                                      start=False, stop=False, skip_group_check=True)
                        if t:
                            pe.matmul(c_bank[:, 0:4 * win], identb, cmask[min(br, 0)],
                                      start=True, stop=False, skip_group_check=True)
                            for h in range(4):
                                pe.matmul(c_bank[:, h * win:(h + 1) * win], selm[:, h * P:(h + 1) * P],
                                          mT[:, n % 2, 0:win], start=False, stop=False, skip_group_check=True)
                        if A:
                            if t:
                                pe.matmul(c_bank[:, 0:4 * win], kA[:, g, q0 - P:q0], qA[:, :, q0:q0 + win],
                                          start=False, stop=True, skip_group_check=True)
                            mm = pe.matmul(t_bank, kA[:, g, q0:q0 + P], qA[:, :, q0:q0 + P], start=False, stop=True,
                                           skip_group_check=True)
                        else:
                            if t:
                                for h in range(4):
                                    pe.matmul(c_bank[:, h * win:(h + 1) * win], qk[rows, 4 + h, q0 - P:q0],
                                              qk[rows, h, q0:q0 + win], start=False, stop=(h == 3),
                                              skip_group_check=True)
                            for h in range(4):
                                mm = pe.matmul(t_bank[:, h * P:(h + 1) * P], qk[rows, 4 + h, q0:q0 + P],
                                               qk[rows, h, q0:q0 + P], start=False, stop=(h == 3),
                                               skip_group_check=True)
                        mm.then_inc(st_full, 1)

                    def weigh(n):
                        br, t, g = unit(n)
                        pe.wait_ge(exp_done, n + 1)
                        taken(pe, values_use(br, t))
                        if br < 0:
                            if g == 0 and t:
                                pe.wait_ge(ot_rdy, t)
                            rows = slice(32 * g, 32 * g + 32)
                            mm = pe.matmul(o_bank[rows, :], vA[:, t, g, :], pm[:, n % 2, :], start=True, stop=(t == 0),
                                           skip_group_check=True)
                            if t:
                                dst = o_bank[rows, :].rearrange("p (h q) -> p h q", h=4)[:, :, 0:A_WIN]
                                mm = pe.matmul(dst, vA[:, t - 1, g, :], pcor[:, n % 2, 0:4 * A_WIN], start=False,
                                               stop=True, skip_group_check=True)
                        else:
                            if n == A_UNITS:
                                pe.wait_ge(ot_rdy, TILES)
                            else:
                                pe.wait_ge(ob_rdy, n - A_UNITS)
                            cols = slice(B_HD * g, B_HD * (g + 2))
                            for h in range(4):
                                mm = pe.matmul(o_bank[:, h * P:(h + 1) * P], vB[:, t, h, cols],
                                               pm[:, n % 2, h * P:(h + 1) * P], start=(h == 0), stop=(t == 0),
                                               skip_group_check=True)
                            for h in range(4 if t else 0):
                                mm = pe.matmul(o_bank[:, h * P:h * P + B_WIN], vB[:, t - 1, h, cols],
                                               pcor[:, n % 2, h * B_WIN:(h + 1) * B_WIN], start=False, stop=True,
                                               skip_group_check=True)
                        mm.then_inc(pv_done, 1)

                    def attention(br):
                        n0, n1 = FIRST_UNIT[br], LAST_UNIT[br]
                        scores(n0)
                        for n in range(n0, n1 + 1):
                            if n < n1:
                                scores(n + 1)
                            turn_max(n)
                            if n > n0:
                                weigh(n - 1)
                            key_scores(n)
                        weigh(n1)

                    def layernorm(name, src, ready):
                        u = USE0[name]
                        for c in range(CHUNKS):
                            ready(c)
                            product(u + c, [(center_s[:, :], src(c))])
                        for c in range(CHUNKS):
                            taken(pe, u + c)
                            product(u + CHUNKS + c, [(ones_s[:, 0:P], sq[:, c, :])])

                    for c in range(CHUNKS):
                        for w in range(2):
                            i = USE0["in"] + 2 * c + w
                            use_wait(pe, i)
                            pe.wait_ge(tok_norm, TILES * w + (c + 1) * TPC)
                            for tt in range(TPC):
                                t = c * TPC + tt
                                tok = (xn_tok if w == 0 else h_tok)[:, t, :]
                                mm = pe.transpose(bank[:, i % RING, tt * P:(tt + 1) * P], tok, ident_s[:, :])
                            mm.then_inc(mm_full, 1)
                    u = USE0["a_proj"]
                    for c in range(CHUNKS):
                        taken(pe, USE0["in"] + 2 * c + 1)
                        for k in range(5):
                            w0 = WA_Q + k * P if k < 4 else WA_K
                            w1_ = WA_QR + k * P if k < 4 else WA_KR
                            product(u + c * 10 + 2 * k, [(wa_s[:, w0:w0 + P], hT[:, cc(c)])])
                            product(u + c * 10 + 2 * k + 1, [(wa_s[:, w1_:w1_ + P], hT[:, cc(c)])])
                    use_wait(pe, u + 20)
                    for t in range(TILES):
                        mm = pe.matmul(bank[:, (u + 20) % RING, t * 32:(t + 1) * 32], hT[:, t * P:(t + 1) * P],
                                       wa_s[:, WA_V:WA_V + 32], start=True, stop=True)
                    mm.then_inc(mm_full, 1)
                    attention(-1)
                    for i in range(8):
                        pe.wait_ge(rec_rdy, (i // 4 + 1) * TPC * A_GRP)
                        product(USE0["a_norm"] + i, [(pick_s[:, :], rec[:, i % 4, cc(i // 4)])])
                    for c in range(CHUNKS):
                        for j in range(4):
                            taken(pe, USE0["a_norm"] + 4 * c + j)
                        product(USE0["a_wo"] + c, [(wo_s[:, j, :], oT[:, j, cc(c)]) for j in range(4)])
                    layernorm("a_ln", lambda c: aT[:, cc(c)], lambda c: taken(pe, USE0["a_wo"] + c))
                    u = USE0["a_ffn"]
                    for c in range(CHUNKS):
                        pe.wait_ge(hn_rdy, c + 1)
                        for f in range(4):
                            product(u + c * 5 + f, [(wf1_s[:, f * P:(f + 1) * P], hT[:, cc(c)])])
                        for f in range(4):
                            taken(pe, u + c * 5 + f)
                        product(u + c * 5 + 4, [(wf2_s[:, f, :], oT[:, f, cc(c)]) for f in range(4)])

                    for l in range(LAYERS):
                        u = USE0[f"proj{l}"]

                        def sum_squares(c, k):
                            i = u + c * 20 + 2 * k
                            j = pair(l, c, k)
                            taken(pe, i)
                            for tt in range(TPC):
                                mm = pe.matmul(bank[:, 4 + c, tt * 16 + 2 * k:tt * 16 + 2 * k + 2],
                                               sq[:, j % 2, tt * P:(tt + 1) * P], ones_s[:, P:P + 2],
                                               start=True, stop=True)
                            mm.then_inc(ss_done, 1)

                        def turn_norms(c):
                            pe.wait_ge(rsp_rdy, l * CHUNKS + c + 1)
                            for tt in range(TPC):
                                mm = pe.transpose(bank[0:48, 6 + c, tt * 64:(tt + 1) * 64].bitcast(BF16),
                                                  rsp[:, c, tt, :], identb)
                            mm.then_inc(rt_full, 1)

                        for c in range(CHUNKS):
                            pe.wait_ge(shift_rdy, l * 4 + c + 1)
                            for k in range(B_QK):
                                product(u + c * 20 + 2 * k, [(wb_s[:, l, k * P:(k + 1) * P], hT[:, cc(c)])])
                                product(u + c * 20 + 2 * k + 1,
                                        [(wb_s[:, l, 1024 + k * P:1024 + (k + 1) * P], hT[:, cc(c)])])
                                if k:
                                    sum_squares(c, k - 1)
                                if c and k == 6:
                                    turn_norms(0)
                            for tt in range(TPC):
                                t = c * TPC + tt
                                product(u + c * 20 + 16 + tt, [(hT[:, t * P:(t + 1) * P], wb_s[:, l, 2048:2560])])
                                if tt == 0:
                                    sum_squares(c, B_QK - 1)
                        turn_norms(1)
                        for c in range(CHUNKS):
                            pe.wait_ge(rt_rdy, l * CHUNKS + c + 1)
                            for k in range(B_QK):
                                product(USE0[f"norm{l}"] + c * 8 + k, [(seln[:, k * P:(k + 1) * P], rT[:, c, :])])
                        attention(l)
                        for c in range(CHUNKS):
                            pe.wait_ge(on_rdy, (l * TILES + (c + 1) * TPC) * 2)
                            product(USE0[f"wo{l}"] + c, [(wob_s[:, l, f, :], oT[:, f, cc(c)]) for f in range(4)])
                        layernorm(f"ln{l}", lambda c: hT[:, cc(c)],
                                  lambda c: pe.wait_ge(shift_rdy, l * 4 + 2 + c + 1))
                        u = USE0[f"ffn{l}"]
                        for c in range(CHUNKS):
                            pe.wait_ge(hn_rdy, (l + 1) * CHUNKS + c + 1)
                            for f, (s, w) in enumerate(HID_T):
                                product(u + c * 7 + 2 * f, [(w1_s[:, l, s:s + w], hT[:, cc(c)])])
                                product(u + c * 7 + 2 * f + 1, [(w1_s[:, l, HID + s:HID + s + w], hT[:, cc(c)])])
                            for f in range(3):
                                taken(pe, u + c * 7 + 2 * f)
                            product(u + c * 7 + 6, [(w2_s[0:w, l, f, :], oT[0:w, f, cc(c)])
                                                    for f, (s, w) in enumerate(HID_T)])
                    for c in range(CHUNKS):
                        i = USE0["out"] + c
                        pe.wait_ge(fin_rdy, c + 1)
                        use_wait(pe, i)
                        for tt in range(TPC):
                            t = c * TPC + tt
                            mm = pe.transpose(bank[:, i % RING, tt * P:(tt + 1) * P], aT[:, t * P:(t + 1) * P],
                                              ident_s[:, :])
                        mm.then_inc(mm_full, 1)

                @block.scalar
                def _(act):
                    def attention(br):
                        A = br < 0
                        win = A_WIN if A else B_WIN
                        scale = A_HD ** -0.5 if A else 8.0

                        def copy_max(n):
                            act.wait_ge(mt_full, n + 1)
                            if n >= 2:
                                act.wait_ge(st_full, n - 1)
                            act.activation(mT[0:8, n % 2, :], x_bank[0:8, 0:64].bitcast(BF16), ACT.Copy)\
                               .then_inc(mt_rdy, 1)

                        def copy_heads(t):
                            act.wait_ge(pv_done, (t + 1) * A_KV)
                            act.activation(oT[:, :, t * P:(t + 1) * P],
                                           o_bank.rearrange("p (f q) -> p f q", f=4), ACT.Copy).then_inc(ot_rdy, 1)

                        def copy_out(n):
                            _, t, g = unit(n)
                            own, other = slice(64 * g, 64 * g + 64), slice(64 * (1 - g), 64 * (1 - g) + 64)
                            act.wait_ge(pv_done, n + 1)
                            if br * TILES + t >= 2:
                                act.wait_ge(on_rdy, (br * TILES + t - 1) * 2)
                            act.activation(oT[own, :, t * P:(t + 1) * P],
                                           o_bank[own, :].rearrange("p (f q) -> p f q", f=4), ACT.Copy)
                            act.activation(sums[own, t % 2, :], o_bank[other, :], ACT.Copy).then_inc(ob_rdy, 1)

                        for n in range(FIRST_UNIT[br], LAST_UNIT[br] + 1):
                            _, t, g = unit(n)
                            copy_max(n)
                            if not A and n > FIRST_UNIT[br]:
                                copy_out(n - 1)
                            act.wait_ge(st_full, n + 1)
                            if n >= 2:
                                act.wait_ge(pv_done, n - 1)
                            if t:
                                act.activation(pcor[:, n % 2, 0:4 * win], c_bank[:, 0:4 * win], ACT.Exp, scale=scale)
                            act.activation(pm[:, n % 2, :], t_bank, ACT.Exp, scale=scale).then_inc(exp_done, 1)
                            if A and g == 0 and t:
                                copy_heads(t - 1)
                        if A:
                            copy_heads(TILES - 1)
                        else:
                            copy_out(LAST_UNIT[br])

                    def layernorm(name):
                        u = USE0[name]
                        for c in range(CHUNKS):
                            act.wait_ge(mm_full, u + c + 1)
                            act.activation(raw[:, c, :], bank[:, (u + c) % RING, :], ACT.Copy).then_inc(raw_rdy, 1)
                            act.activation(sq[:, c, :], bank[:, (u + c) % RING, :], ACT.Square)\
                               .then_inc(drained[(u + c) % RING], 1)
                        for c in range(CHUNKS):
                            i = u + CHUNKS + c
                            act.wait_ge(mm_full, i + 1)
                            act.activation(pc[:, c, :], bank[:, i % RING, :], ACT.Ln, bias=eps_s[:, 0:1])\
                               .then_inc(drained[i % RING], 1)
                        for c in range(CHUNKS):
                            taken(act, u + CHUNKS + c)
                            act.activation(ps_[:, c, :], pc[:, c, :], ACT.Exp, scale=-0.5).then_inc(rstd_rdy, 1)

                    for c in range(CHUNKS):
                        for w in range(2):
                            i = USE0["in"] + 2 * c + w
                            act.wait_ge(mm_full, i + 1)
                            act.activation(xc(c) if w == 0 else hT[:, cc(c)], bank[:, i % RING, :], ACT.Copy)\
                               .then_inc(drained[i % RING], 1)
                    for j in range(10):
                        act.wait_ge(sum_rdy, j + 1)
                        if j >= 2:
                            act.wait_ge(split_rdy, j - 1)
                        act.activation(hiA[:, j % 2, :], raw[:, j % 2, :], ACT.Copy).then_inc(hi_rdy, 1)
                    i = USE0["a_proj"] + 20
                    act.wait_ge(mm_full, i + 1)
                    act.activation(vA[:, :, :, 0:A_HD],
                                   bank[:, i % RING, 0:256].rearrange("p (t g d) -> p t g d", t=TILES, g=A_KV),
                                   ACT.Copy).then_inc(drained[i % RING], 1)
                    attention(-1)
                    layernorm("a_ln")
                    u = USE0["a_ffn"]
                    for c in range(CHUNKS):
                        for f in range(4):
                            i = u + c * 5 + f
                            act.wait_ge(mm_full, i + 1)
                            act.activation(oT[:, f, cc(c)], bank[:, i % RING, :], ACT.Gelu,
                                           bias=bias[:, V_BF1 + f:V_BF1 + f + 1]).then_inc(drained[i % RING], 1)
                    for l in range(LAYERS):
                        u = USE0[f"proj{l}"]

                        def copy_norms(c):
                            act.wait_ge(rt_full, l * CHUNKS + c + 1)
                            act.activation(rT[:, c, :], bank[0:48, 6 + c, 0:256].bitcast(BF16), ACT.Copy)\
                               .then_inc(rt_rdy, 1)

                        for c in range(CHUNKS):
                            for k in range(B_QK):
                                i, j = u + c * 20 + 2 * k, pair(l, c, k)
                                jb = j - 10
                                act.wait_ge(mm_full, i + 1)
                                if jb >= 2:
                                    act.wait_ge(prod_rdy, jb - 1)
                                act.activation(raw[:, j % 2, :], bank[:, i % RING, :], ACT.Copy).then_inc(raw_rdy, 1)
                                if jb >= 2:
                                    act.wait_ge(ss_done, jb - 1)
                                act.activation(sq[:, j % 2, :], bank[:, i % RING, :], ACT.Square)\
                                   .then_inc(drained[i % RING], 1)
                                if c and k == 7:
                                    copy_norms(0)
                            for tt in range(TPC):
                                i, t = u + c * 20 + 16 + tt, c * TPC + tt
                                act.wait_ge(mm_full, i + 1)
                                act.wait_ge(pv_done, FIRST_UNIT[l])
                                v = bank[:, i % RING, :].rearrange("p (h g d) -> p h g d", h=4, g=2)
                                act.activation(vB[:, t, :, :].rearrange("p h (g d) -> p h g d", g=3)[:, :, 0::2, :],
                                               v, ACT.Copy).then_inc(drained[i % RING], 1)
                        copy_norms(1)
                        attention(l)
                        layernorm(f"ln{l}")
                        u = USE0[f"ffn{l}"]
                        for c in range(CHUNKS):
                            for f, (s, w) in enumerate(HID_T):
                                i = u + c * 7 + 2 * f + 1
                                n = (l * CHUNKS + c) * 3 + f
                                act.wait_ge(mm_full, i + 1)
                                if f == 2:
                                    taken(act, i - 5)
                                elif c:
                                    taken(act, i - 6)
                                bc = V_L + l * VL_N + VL_B1 + 3 + f
                                act.activation(gel[0:w, n % 2, :], bank[0:w, i % RING, :], ACT.Gelu,
                                               bias=bias[0:w, bc:bc + 1]).then_inc(drained[i % RING], 1)

                @block.vector
                def _(dve):
                    steps = [0]

                    def link(ins):
                        steps[0] += 1
                        ins.then_inc(v_link, 1)
                        dve.wait_ge(v_link, steps[0])

                    def token_norm(src, dst):
                        for t in range(TILES):
                            ins = dve.bn_stats(stat[:, t, :], src[:, t, :])
                        link(ins)
                        for t in range(TILES):
                            ins = dve.bn_aggr(mv[:, t, :], stat[:, t, :])
                        link(ins)
                        inv_root(mv[:, :, 1], EPS, ALU.add, TILES)
                        for t in range(TILES):
                            dve.tensor_scalar(dst[:, t, :], src[:, t, :], mv[:, t, 0:1], nw[:, 1, t:t + 1],
                                              ALU.subtract, ALU.mult).then_inc(tok_norm, 1)

                    def inv_root(src, c, op, n):
                        v, y, t, s = (nw[:, r, 0:n] for r in range(4))
                        link(dve.tensor_scalar(v, src, c, None, op))
                        link(dve.tensor_scalar(y.bitcast(I32), v.bitcast(I32), -0.5, float(0x5F3759DF), ALU.mult,
                                               ALU.add))
                        for _ in range(4):
                            link(dve.tensor_tensor(t, y, y, ALU.mult))
                            link(dve.scalar_tensor_tensor(s, t, -0.5, v, ALU.mult, ALU.mult))
                            link(dve.scalar_tensor_tensor(y, s, 1.5, y, ALU.add, ALU.mult))

                    def rotate(br, c, k, i, ct, st, gc=None, gs=None):
                        j = pair(br, c, k)
                        A = br < 0
                        if j >= 2:
                            dve.wait_ge(sum_rdy, j - 1)
                        if A:
                            bq, bqr = (V_BQ + k, V_BQR + k) if k < 4 else (V_BK, V_BKR)
                            dve.wait_ge(mm_full, i + 1)
                            dve.scalar_tensor_tensor(pc[:, j % 2, :], bank[:, i % RING, :], bias[:, bq:bq + 1], ct,
                                                     ALU.add, ALU.mult).then_inc(drained[i % RING], 1)
                            dve.wait_ge(mm_full, i + 2)
                            dve.scalar_tensor_tensor(ps_[:, j % 2, :], bank[:, (i + 1) % RING, :],
                                                     bias[:, bqr:bqr + 1], st, ALU.add, ALU.mult)\
                               .then_inc(drained[(i + 1) % RING], 1)
                        else:
                            raws = RAW0[br] + c * 8 + k
                            dve.wait_ge(mm_full, i + 2)
                            dve.scalar_tensor_tensor(ps_[:, j % 2, :], bank[:, (i + 1) % RING, :], gs, st, ALU.mult,
                                                     ALU.mult).then_inc(drained[(i + 1) % RING], 1)
                            dve.wait_ge(raw_rdy, raws + 1)
                            dve.scalar_tensor_tensor(pc[:, j % 2, :], raw[:, j % 2, :], gc, ct, ALU.mult,
                                                     ALU.mult).then_inc(prod_rdy, 1)

                    RAW0 = {0: 2, 1: 2 + 16 + 2}
                    RAWLN = {"a_ln": 0, "ln0": 2 + 16, "ln1": 2 + 16 + 2 + 16}

                    def attention(br):
                        A = br < 0
                        win = A_WIN if A else B_WIN

                        def maxima(n):
                            _, t, _ = unit(n)
                            w = P if t == 0 else P + win
                            dve.wait_ge(sc_full, n + 1)
                            if n >= 2:
                                dve.wait_ge(mt_full, n - 1)
                            link(dve.tensor_reduce(mx[:, n % 2, :],
                                                   s_bank[n % 2][:, :, 0:2 * w].rearrange("p b (h w) -> p b h w", h=2),
                                                   AX_X, ALU.max))
                            link(dve.tensor_scalar(negm[:, n % 2, 0:4], mx[:, n % 2, :], -1.0, None, ALU.mult))
                            dve.scalar_tensor_tensor(negm[:, n % 2, 4:8], mx[:, n % 2, :], -1.0, negm[:, n % 2, 0:4],
                                                     ALU.mult, ALU.subtract).then_inc(max_rdy, 1)

                        def invert(m):
                            t, h = divmod(m, A_GRP)
                            dve.wait_ge(ot_rdy, t + 1)
                            r = rec[:, h, t * P:(t + 1) * P]
                            link(dve.tensor_scalar(r, oT[:, h, t * P:(t + 1) * P], 0.5, None, ALU.max))
                            dve.reciprocal(r, r).then_inc(rec_rdy, 1)

                        def normalise(m):
                            t, half = divmod(m, 2)
                            dve.wait_ge(ob_rdy, (br * TILES + t + 1) * 2)
                            q = slice(256 * half, 256 * (half + 1))
                            o = oT[:, 2 * half:2 * half + 2, t * P:(t + 1) * P]
                            link(dve.reciprocal(rl[:, q], sums[:, t % 2, q]))
                            dve.tensor_tensor(o, o, rl[:, q].rearrange("p (f q) -> p f q", f=2), ALU.mult)\
                               .then_inc(on_rdy, 1)

                        maxima(FIRST_UNIT[br])
                        step, lag, count = (invert, A_GRP + 1, A_UNITS) if A else (normalise, 3, B_UNITS)
                        for n in range(FIRST_UNIT[br], LAST_UNIT[br] + 1):
                            m = n - FIRST_UNIT[br]
                            if n < LAST_UNIT[br]:
                                maxima(n + 1)
                            if m >= lag:
                                step(m - lag)
                        for m in range(count - lag, count):
                            step(m)

                    def layernorm(name):
                        for c in range(CHUNKS):
                            dve.wait_ge(raw_rdy, RAWLN[name] + c + 1)
                            dve.wait_ge(rstd_rdy, ln_n(name, c) + 1)
                            dve.tensor_tensor(hT[:, cc(c)], raw[:, c, :], ps_[:, c, :], ALU.mult).then_inc(hn_rdy, 1)

                    def shift():
                        for c in range(CHUNKS):
                            dve.tensor_copy(hT[0:64, cc(c)], xT[0:64, 1 + c * CH:1 + (c + 1) * CH])
                            dve.tensor_copy(hT[64:128, cc(c)], xT[64:128, c * CH:(c + 1) * CH])\
                               .then_inc(shift_rdy, 1)

                    dve.wait_ge(x_in, 16)
                    token_norm(x_tok, xn_tok)
                    dve.wait_ge(tok_norm, TILES)
                    token_norm(xn_tok, h_tok)
                    dve.wait_ge(kz_rdy, 1)
                    u = USE0["a_proj"]

                    def split(c, k):
                        j = pair(-1, c, k)
                        dve.wait_ge(hi_rdy, j + 1)
                        if k < 4:
                            dve.scalar_tensor_tensor(qA[:, k, cc(c)], hiA[:, j % 2, :].bitcast(F32),
                                                     vec_s[:, V_SQ:V_SQ + 1], raw[:, j % 2, :], ALU.mult,
                                                     ALU.add).then_inc(split_rdy, 1)
                            return
                        for g in range(A_KV):
                            r = slice(32 * g, 32 * g + 32)
                            ins = dve.scalar_tensor_tensor(kA[r, g, cc(c)], hiA[r, j % 2, :].bitcast(F32),
                                                           vec_s[r, V_SK:V_SK + 1], raw[r, j % 2, :], ALU.mult,
                                                           ALU.add)
                        ins.then_inc(split_rdy, 1)

                    for j in range(11):
                        if j < 10:
                            c, k = divmod(j, 5)
                            rotate(-1, c, k, u + c * 10 + 2 * k, tab_s[:, 4, cc(c)], tab_s[:, 5, cc(c)])
                        if j:
                            split(*divmod(j - 1, 5))
                    attention(-1)
                    for i in range(8):
                        use, o = USE0["a_norm"] + i, oT[:, i % 4, cc(i // 4)]
                        dve.wait_ge(mm_full, use + 1)
                        dve.tensor_tensor(o, bank[:, use % RING, :], o, ALU.mult).then_inc(drained[use % RING], 1)
                    for c in range(CHUNKS):
                        i = USE0["a_wo"] + c
                        dve.wait_ge(mm_full, i + 1)
                        dve.scalar_tensor_tensor(aT[:, cc(c)], bank[:, i % RING, :], bias[:, V_BO:V_BO + 1], xc(c),
                                                 ALU.add, ALU.add).then_inc(drained[i % RING], 1)
                    layernorm("a_ln")
                    for c in range(CHUNKS):
                        i = USE0["a_ffn"] + c * 5 + 4
                        dve.wait_ge(mm_full, i + 1)
                        dve.scalar_tensor_tensor(aT[:, cc(c)], bank[:, i % RING, :], vec_s[:, V_BF2:V_BF2 + 1],
                                                 aT[:, cc(c)], ALU.add, ALU.add).then_inc(drained[i % RING], 1)
                    for l in range(LAYERS):
                        vl = V_L + l * VL_N
                        shift()
                        u = USE0[f"proj{l}"]
                        def norms(c):
                            dve.wait_ge(ss_done, (l * CHUNKS + c + 1) * B_QK)
                            inv_root(bank[:, 4 + c, 0:64], 1e-24, ALU.max, 64)
                            y, r_ = nw[:, 1, :], nw[:, 2, :]
                            part = [rsp[:, c, :, 16 * m:16 * (m + 1)] for m in range(3)]
                            y, r_ = (z.rearrange("p (t k) -> p t k", t=TPC) for z in (y, r_))
                            link(dve.tensor_copy(part[0], y))
                            link(dve.tensor_tensor(r_, y, part[0], ALU.subtract))
                            link(dve.tensor_copy(part[1], r_))
                            dve.tensor_tensor(part[2], r_, part[1], ALU.subtract).then_inc(rsp_rdy, 1)

                        for c in range(CHUNKS):
                            for k in range(B_QK):
                                if c and k == 3:
                                    norms(0)
                                r = 0 if k < 4 else 2
                                g = vl + VL_QS + r
                                rotate(l, c, k, u + c * 20 + 2 * k, tab_s[:, r, cc(c)], tab_s[:, r + 1, cc(c)],
                                       vec_s[:, g:g + 1], vec_s[:, g + 1:g + 2])
                        norms(1)
                        for c in range(CHUNKS):
                            for k in range(B_QK):
                                i = USE0[f"norm{l}"] + c * 8 + k
                                dve.wait_ge(sum_rdy, pair(l, c, k) + 1)
                                dve.wait_ge(mm_full, i + 1)
                                dve.tensor_tensor(qk[:, k, cc(c)], bank[:, i % RING, :], qk[:, k, cc(c)], ALU.mult)\
                                   .then_inc(drained[i % RING], 1)
                        attention(l)
                        for c in range(CHUNKS):
                            i = USE0[f"wo{l}"] + c
                            dve.wait_ge(mm_full, i + 1)
                            dve.tensor_tensor(xc(c), bank[:, i % RING, :], xc(c), ALU.add)\
                               .then_inc(drained[i % RING], 1)
                            taken(dve, i)
                        shift()
                        layernorm(f"ln{l}")
                        u = USE0[f"ffn{l}"]
                        for c in range(CHUNKS):
                            for f, (s, w) in enumerate(HID_T):
                                i = u + c * 7 + 2 * f
                                n = (l * CHUNKS + c) * 3 + f
                                dve.wait_ge(mm_full, i + 1)
                                taken(dve, i + 1)
                                bc = vl + VL_B1 + f
                                dve.scalar_tensor_tensor(oT[0:w, f, cc(c)], bank[0:w, i % RING, :],
                                                         bias[0:w, bc:bc + 1], gel[0:w, n % 2, :], ALU.add,
                                                         ALU.mult).then_inc(drained[i % RING], 1)
                            i = u + c * 7 + 6
                            dve.wait_ge(mm_full, i + 1)
                            dve.scalar_tensor_tensor(xc(c), bank[:, i % RING, :],
                                                     vec_s[:, vl + VL_B2:vl + VL_B2 + 1], xc(c), ALU.add,
                                                     ALU.add).then_inc(drained[i % RING], 1)
                            taken(dve, i)
                    for c in range(CHUNKS):
                        dve.tensor_tensor(aT[:, cc(c)], aT[:, cc(c)], xc(c), ALU.add).then_inc(fin_rdy, 1)
                    for c in range(CHUNKS):
                        i = USE0["out"] + c
                        dve.wait_ge(mm_full, i + 1)
                        tt = slice(c * TPC, (c + 1) * TPC)
                        dve.tensor_tensor(x_tok[:, tt, :], bank[:, i % RING, :].rearrange("p (t d) -> p t d", d=D),
                                          x_tok[:, tt, :], ALU.add).then_inc(out_rdy, 1)

            nc.all_engine_barrier(sems_to_clear=range(first, last + 1))


def host_constants():
    import numpy as np
    f = np.float32
    pos = np.arange(T, dtype=f)
    half = np.arange(0, B_HD, 2, dtype=f)
    inv = (f(1.0) / np.power(f(10000.0), half / f(B_HD))).astype(f)
    fr = (pos[:, None] * inv[None, :]).astype(f)
    fr = np.concatenate([fr, fr], axis=-1)
    base = ((half + f(0.4 * B_HD)) / f(1.4 * B_HD)).astype(f)
    power = ((pos - f(T // 2)) / f(B_WIN // 2)).astype(f)
    sc = np.power(base[None, :], power[:, None]).astype(f)
    sc = np.concatenate([sc, sc], axis=-1)
    sign = np.where(np.arange(B_HD) < B_HD // 2, f(-1), f(1))
    cos, sin = np.cos(fr).astype(f), np.sin(fr).astype(f) * sign
    tabs = np.zeros((P, 6, T), f)
    for r, tab in enumerate((cos * sc, sin * sc, cos / sc, sin / sc)):
        tabs[:, r, :] = np.concatenate([tab, tab], axis=1).T
    th = (f(1.0) / np.power(f(10000.0), np.arange(A_HD // 2, dtype=f) / f(A_HD // 2))).astype(f)
    fr = (pos[:, None] * th[None, :]).astype(f)
    for row in range(P):
        d = row % A_HD
        a = fr[:, d % (A_HD // 2)]
        tabs[row, 4] = np.cos(a)
        tabs[row, 5] = np.sin(a) * (f(-1) if d < A_HD // 2 else f(1))
    ident = np.eye(P, dtype=f)
    center = (ident - f(1.0 / P)).astype(f)
    ones = np.zeros((P, P + 2), f)
    ones[:, :P] = 1.0 / P
    ones[:64, P] = 1
    ones[64:, P + 1] = 1
    pick = np.zeros((P, P), f)
    for g in range(A_KV):
        pick[32 * g + A_HD, 32 * g:32 * g + 32] = 1
    r = np.arange(P)

    def allow(diff, win, strict):
        ok = (diff >= 0) & ((diff < win) if strict else (diff <= win))
        return np.where(ok, f(0), f(-1e30))

    parts = [ident]
    for win, s in ((A_WIN, True), (B_WIN, False)):
        parts.append(np.tile(allow(r[:, None] - (np.arange(P + win)[None, :] - win), win, s), (1, 2)))
    for win, s in ((A_WIN, True), (B_WIN, False)):
        parts.append(np.tile(allow(r[:, None] - r[None, :], win, s), (1, 2)))
    for win, s in ((A_WIN, True), (B_WIN, False)):
        parts.append(np.tile(allow(r[None, :] - r[:, None], win, s), (1, 4)))
    for win, s in ((A_WIN, True), (B_WIN, False)):
        parts.append(np.tile(allow(P + np.arange(win)[None, :] - r[:, None], win, s), (1, 4)))
    selm = np.zeros((P, 4, P), f)
    for h in range(4):
        selm[h, h] = 1
        selm[4 + h, h] = 1
    seln = np.zeros((P, B_QK, P), f)
    for k in range(B_QK):
        for m in range(3):
            seln[16 * m + 2 * k, k, :64] = 1
            seln[16 * m + 2 * k + 1, k, 64:] = 1
    parts += [selm.reshape(P, -1), seln.reshape(P, -1)]
    cbf = np.concatenate(parts, axis=1).astype(np.dtype("bfloat16"))
    return dict(tabs=tabs, ident=ident, center=center, ones=ones, pick=pick, cbf=cbf)


def host_layout(i):
    import numpy as np
    f = np.float32
    n = {k[3:]: np.asarray(v) for k, v in i.items()}
    wq, wk, wv = n["attn_Wq"], n["attn_Wk"], n["attn_Wv"]
    bq, bk, bv = n["attn_bq"], n["attn_bk"], n["attn_bv"]
    wa = np.zeros((P, WA_N), f)
    vec = np.zeros((P, V_N), f)
    wo = np.zeros((P, A_GRP, D), f)
    wvr = np.zeros((P, P), f)
    turn = (np.arange(A_HD) + A_HD // 2) % A_HD
    for g in range(A_KV):
        dup = [(32 * g + A_HD * m) for m in range(4)]
        for j in range(A_GRP):
            h = A_GRP * g + j
            for off, voff, cl in ((WA_Q, V_BQ, A_HD * h + np.arange(A_HD)), (WA_QR, V_BQR, A_HD * h + turn)):
                for r in dup:
                    wa[:, off + j * P + r:off + j * P + r + A_HD] = wq[:, cl]
                    vec[r:r + A_HD, voff + j] = bq[cl]
            wo[32 * g:32 * g + A_HD, j] = n["attn_Wo"][A_HD * h:A_HD * (h + 1)]
        for off, voff, cl in ((WA_K, V_BK, A_HD * g + np.arange(A_HD)), (WA_KR, V_BKR, A_HD * g + turn)):
            for r in dup:
                wa[:, off + r:off + r + A_HD] = wk[:, cl]
                vec[r:r + A_HD, voff] = bk[cl]
        wvr[:, 32 * g:32 * g + A_HD] = wv[:, A_HD * g:A_HD * (g + 1)]
        vec[32 * g:32 * g + A_HD, V_BVR] = bv[A_HD * g:A_HD * (g + 1)]
    wa[:, WA_V:] = wv
    blk = np.arange(P) % 32 // A_HD
    vec[:, V_SQ] = np.where(blk >= 2, f(-1), f(0))
    vec[:, V_SK] = np.where(blk % 2 == 1, f(-1), f(0))
    for c, k in ((V_G1, "attn_g1"), (V_B1, "attn_b1"), (V_G2, "attn_g2"), (V_B2, "attn_b2"), (V_BO, "attn_bo"),
                 (V_BF2, "attn_bf2")):
        vec[:, c] = n[k]
    vec[:, V_BF1:V_BF1 + 4] = n["attn_bf1"].reshape(4, P).T
    wf2 = np.ascontiguousarray(n["attn_Wf2"].reshape(4, P, D).transpose(1, 0, 2))
    wqkv = n["ffn_wqkv"]
    turn = (np.arange(B_HD) + B_HD // 2) % B_HD
    cols = np.concatenate([B_HD * h + turn for h in range(2 * B_H)])
    wb = np.ascontiguousarray(np.concatenate([wqkv[:, :, :1024], wqkv[:, :, cols], wqkv[:, :, 1024:]], axis=2)
                              .transpose(1, 0, 2))
    wob = np.ascontiguousarray(n["ffn_wo"].reshape(LAYERS, 4, P, D).transpose(2, 0, 1, 3))
    w1 = np.ascontiguousarray(n["ffn_w1"].transpose(1, 0, 2))
    w2 = np.zeros((P, LAYERS, 3, P), f)
    for l in range(LAYERS):
        o = V_L + l * VL_N
        vec[:, o + VL_G], vec[:, o + VL_B], vec[:, o + VL_B2] = n["ffn_ln_g"][l], n["ffn_ln_b"][l], n["ffn_b2"][l]
        for q, (k, t) in enumerate((("q", 0), ("q", 1), ("k", 0), ("k", 1))):
            s = n[f"ffn_{k}_scale"][l]
            vec[:, o + VL_QS + q] = np.concatenate([s[turn] if t else s] * 2)
        for hf in range(2):
            for t, (s, w) in enumerate(HID_T):
                vec[:w, o + VL_B1 + 3 * hf + t] = n["ffn_b1"][l, hf * HID + s:hf * HID + s + w]
        for t, (s, w) in enumerate(HID_T):
            w2[:w, l, t] = n["ffn_w2"][l, s:s + w]
    return dict(x=n["attn_x"], wa=wa, wo=wo, wf1=n["attn_Wf1"], wf2=wf2, wvr=wvr, vec=vec, wb=wb,
                wob=wob, w1=w1, w2=w2)


def kernel(**inputs):
    import numpy as np
    import concourse.bacc as bacc
    from concourse.bass_utils import run_bass_kernel_spmd

    nc = bacc.Bacc("TRN2", target_bir_lowering=False, num_devices=1)
    arrays = {k: np.ascontiguousarray(v) for k, v in {**host_layout(inputs), **host_constants()}.items()}
    args = {k: nc.dram_tensor(k, v.shape, mybir.dt.from_np(v.dtype), kind="ExternalInput").ap()
            for k, v in arrays.items()}
    out = nc.dram_tensor("out", (BATCH, T, D), F32, kind="ExternalOutput").ap()
    program(nc, out=out, **args)
    return run_bass_kernel_spmd(nc, [arrays], core_ids=[0]).results[0]["out"]
```

```python
from contextlib import ExitStack

import concourse.bass as bass
from concourse import mybir

F32 = mybir.dt.float32
F32R = mybir.dt.float32r
BF16 = mybir.dt.bfloat16
I32 = mybir.dt.int32
ALU = mybir.AluOpType
ACT = mybir.ActivationFunctionType
AX_X = mybir.AxisListType.X

P = 128
BATCH, T, D = 4, 1024, 128
TILES = T // P
CH = 512
CHUNKS = T // CH
TPC = CH // P
LAYERS = 2
A_KV, A_GRP, A_HD, A_WIN, A_FF = 4, 4, 8, 32, 4
B_H, B_HD, B_WIN = 8, 64, 64
B_QK = 2 * B_H * B_HD // P
HID = 341
HID_T = [(0, 128), (128, 128), (256, HID - 256)]
EPS = 1e-5

A_UNITS = TILES * A_KV
B_UNITS = TILES * B_H // 4
UNITS = A_UNITS + LAYERS * B_UNITS

WA_Q, WA_QR, WA_K, WA_KR, WA_V = 0, 512, 1024, 1152, 1280
WA_N = 1312
(V_G1, V_B1, V_G2, V_B2, V_BO, V_BF2, V_BVR, V_BQ, V_BQR, V_BK, V_BKR, V_BF1, V_SQ, V_SK, V_SUM, V_HEAD) = (
    0, 1, 2, 3, 4, 5, 6, 7, 11, 15, 16, 17, 21, 22, 23, 24)
V_L = 25
(VL_G, VL_B, VL_B2, VL_QS, VL_B1) = (0, 1, 2, 3, 5)
VL_N = 11
V_N = V_L + LAYERS * VL_N

STAGES = [("in", 4), ("a_proj", 21), ("a_norm", 8), ("a_wo", 2), ("a_ln", 2)]
for _l in range(LAYERS):
    STAGES += [(f"qk{_l}0", 8)] + [("a_ln_mean", 2)] * (_l == 0) + [(f"v{_l}0", 4), (f"qk{_l}1", 16), (f"v{_l}1", 4)]
    STAGES += [(f"norm{_l}", 8), (f"wo{_l}", 2), (f"a_hid{_l}0", 2), (f"ln{_l}", 2), (f"a_hid{_l}1", 2),
               (f"ln{_l}_mean", 2), (f"a_out{_l}", 1), (f"ffn{_l}", 14)]
STAGES += [("out", 2)]
USE0 = {}
_n = 0
for _name, _k in STAGES:
    USE0[_name] = _n
    _n += _k
RING = 4


def qk_use(l, c, k):
    return USE0[f"qk{l}{c}"] + (k if c == 0 or k < 4 else 4 + 3 * (k - 4))


def norm_use(l, c, k):
    return USE0[f"norm{l}"] + k if c else USE0[f"qk{l}1"] + 4 + 3 * (k // 2) + 1 + k % 2


def ffn_use(l, c, k):
    if c == 0:
        return USE0[f"ffn{l}"] + (k if k < 6 else 8)
    return USE0[f"ffn{l}"] + (6 + k if k < 2 else 7 + k)


def unit(n):
    if n < A_UNITS:
        return -1, n // A_KV, n % A_KV
    m = n - A_UNITS
    return m // B_UNITS, m % B_UNITS // 2, m % 2


def program(nc, x, wa, wo, wf1, wf2, wvr, vec, wb, wob, w1, w2, tabs, ident, center, ones, sum_heads, pick, cbf, out):
    ctx = ExitStack()
    with ctx:
        def sb(name, shape, dt=F32):
            return ctx.enter_context(nc.sbuf_tensor(name, shape, dt))

        def sem(name):
            return ctx.enter_context(nc.semaphore(name))

        wa_s = sb("wa_s", [P, WA_N])
        wo_s = sb("wo_s", [P, A_GRP, D])
        wf1_s = sb("wf1_s", [P, A_FF * P])
        wf2_s = sb("wf2_s", [P, A_FF, P])
        vec_s = sb("vec_s", [P, V_N])
        bias = sb("bias", [P, V_N])
        wb_s = sb("wb_s", [P, LAYERS, 1536])
        wob_s = sb("wob_s", [P, LAYERS, 4, P])
        w1_s = sb("w1_s", [P, LAYERS, 2 * HID])
        w2_s = sb("w2_s", [P, LAYERS, 3, P])
        tab_s = sb("tab_s", [P, 6, T])
        ident_s = sb("ident_s", [P, P])
        center_s = sb("center_s", [P, P])
        ones_s = sb("ones_s", [P, P])
        sum_s = sb("sum_s", [P, B_QK, 16])
        pick_s = sb("pick_s", [P, P])
        eps_s = sb("eps_s", [P, 1])
        CB = cbf.shape[1]
        cbf_s = sb("cbf_s", [P, CB], BF16)
        o = 0
        identb = cbf_s[:, 0:128]
        o = 128
        smask = {-1: cbf_s[:, o:o + 320], 0: cbf_s[:, o + 320:o + 704]}
        o += 704
        smask0 = {-1: cbf_s[:, o:o + 256], 0: cbf_s[:, o + 256:o + 512]}
        o += 512
        tmask = {-1: cbf_s[:, o:o + 512], 0: cbf_s[:, o + 512:o + 1024]}
        o += 1024
        cmask = {-1: cbf_s[:, o:o + 128], 0: cbf_s[:, o + 128:o + 384]}
        o += 384
        selm = cbf_s[:, o:o + 512]
        o += 512
        seln = cbf_s[0:48, o:o + 1024]
        o += 1024
        assert o == CB

        x_tok = sb("x_tok", [P, TILES, D])
        xn_tok = sb("xn_tok", [P, TILES, D])
        xn_stat = sb("xn_stat", [P, TILES, 2])
        xT = sb("xT", [P, T + 1])
        aT = sb("aT", [P, T])
        with nc.sbuf_tensor("sums", [P, 2, 512], F32) as sums:
            pass
        hT = sb("hT", [P, T])
        with nc.sbuf_tensor("qA", [P, A_GRP, T], F32R) as qA, nc.sbuf_tensor("kA", [P, A_KV, T], F32R) as kA:
            pass
        qk = sb("qk", [P, B_QK, T])
        vB = sb("vB", [P, TILES, 4, 3 * B_HD])
        vA = sb("vA", [P, TILES, A_KV, 32])
        hA = sb("hA", [P, T])
        oT = sb("oT", [P, 4, T])
        with nc.sbuf_tensor("rec", [P, A_GRP, T], F32) as rec:
            pass
        with nc.sbuf_tensor("qR", [P, 2, 4, P], F32R) as qR, \
                nc.sbuf_tensor("kR", [P, 2, 4, P + B_WIN], F32R) as kR, \
                nc.sbuf_tensor("norm_more", [P, 1, CH], F32) as norm_more:
            pass
        raw = sb("raw", [P, 4, CH])
        rot = sb("rot", [P, 4, CH])
        with nc.sbuf_tensor("rl", [P, 2, 256], F32) as rl:
            pass
        with nc.sbuf_tensor("hiA", [P, 2, CH], F32R) as hiA:
            pass
        sq = sb("sq", [P, 2, CH])
        pc = sb("pc", [P, 2, CH])
        ps_ = sb("ps_", [P, 2, CH])
        with nc.sbuf_tensor("kD", [P, 2, CH], F32R) as kD:
            pass
        with nc.sbuf_tensor("ss", [16, 2, CH], F32) as ss:
            pass
        pm = sb("pm", [P, 2, 512])
        with nc.sbuf_tensor("rT", [48, 2, CH], BF16) as rT:
            pass
        pcor = sb("pcor", [P, 2, 256])
        gel = pm
        stat = sb("stat", [P, TILES, 6])
        mv = sb("mv", [P, TILES, 2])
        nw = sb("nw", [P, 4, 64])
        rsp = sb("rsp", [P, 2, TPC, 48], BF16)
        mx = sb("mx", [P, 2, 4])
        negm = sb("negm", [P, 2, 8], BF16)
        mT = sb("mT", [P, 2, P], BF16)

        bank = ctx.enter_context(nc.psum_tensor("bank", [P, 8, 512], F32))
        s_bank = [bank[:, 0:2, :], bank[:, 2:4, :]]
        t_bank, c_bank, o_bank, x_bank = (bank[:, b, :] for b in (4, 5, 6, 7))

        tab_a_in = sem("rotation_tables_a_loaded")
        tab_b_in = sem("rotation_tables_b_loaded")
        late_in = sem("later_weights_loaded")
        s_load = sem("weights_loaded")
        first_x = sem("first_x_loaded")
        setup_v = sem("setup_vector")
        setup_p = sem("setup_pool")
        setup_mm = sem("setup_products")
        setup_link = sem("setup_step")
        first = s_load.num
        x_in = sem("x_loaded")
        next_in = sem("next_x_loaded")
        round_rdy = sem("q_k_rounded")
        late_scaled = sem("chunk_1_scaled")
        tok_norm = sem("tokens_normed")
        mm_full = sem("product_ready")
        drained = [sem(f"bank{b}_drained") for b in range(RING)]
        raw_rdy = sem("raw_copied")
        prod_rdy = sem("rotary_products")
        sum_rdy = sem("rotated")
        ss_done = sem("squares_summed")
        sums_copied = sem("sums_of_squares_copied")
        sums_turned = sem("sums_of_squares_turned")
        rot_rdy = [sem(f"rows_exchanged{s}") for s in range(4)]
        rsp_rdy = sem("norms_split")
        rt_full = sem("norms_turned")
        rt_rdy = sem("norms_copied")
        shift_rdy = sem("shifted")
        sc_full = sem("scores_ready")
        max_rdy = sem("maxima_ready")
        mt_full = sem("maxima_turned")
        mt_rdy = sem("maxima_copied")
        st_full = sem("key_scores_ready")
        exp_done = sem("probs_ready")
        pv_done = sem("values_weighted")
        on_rdy = sem("heads_normalised")
        hi_rdy = sem("leading_halves")
        split_rdy = sem("halves_laid_out")
        ka_rdy = sem("key_heads_set_apart")
        kz_rdy = sem("keys_zeroed")
        rec_rdy = sem("sums_inverted")
        ob_rdy = sem("heads_and_sums_copied")
        ot_rdy = sem("heads_copied")
        rstd_rdy = sem("rstd_ready")
        hn_rdy = sem("ln_ready")
        fin_rdy = sem("branches_added")
        out_rdy = sem("out_ready")
        out_done = sem("out_stored")
        v_link = sem("vector_step")
        last = v_link.num

        def xc(c):
            return xT[:, 1 + c * CH:1 + (c + 1) * CH]

        def cc(c):
            return slice(c * CH, (c + 1) * CH)

        biases = [(wa_s[:, WA_Q + j * P:WA_Q + (j + 1) * P], V_B1, V_BQ + j) for j in range(4)]
        biases += [(wa_s[:, WA_QR + j * P:WA_QR + (j + 1) * P], V_B1, V_BQR + j) for j in range(4)]
        biases += [(wa_s[:, WA_K:WA_K + P], V_B1, V_BK), (wa_s[:, WA_KR:WA_KR + P], V_B1, V_BKR)]
        biases += [(wf1_s[:, f * P:(f + 1) * P], V_B2, V_BF1 + f) for f in range(4)]
        for l in range(LAYERS):
            for half in range(2):
                for f, (s, w) in enumerate(HID_T):
                    biases.append((w1_s[:, l, half * HID + s:half * HID + s + w], V_L + l * VL_N + VL_B,
                                   V_L + l * VL_N + VL_B1 + half * 3 + f))
        NB = len(biases)
        wvr_s = aT[:, 0:P]

        def tokens(dram, b):
            return dram[bass.ds(b, 1), :, :].rearrange("a (t p) d -> p (a t) d", p=P)

        def linker(dve, semaphore):
            steps = [0]

            def link(ins):
                steps[0] += 1
                ins.then_inc(semaphore, 1)
                dve.wait_ge(semaphore, steps[0])
            return link

        def inv_root(dve, link, src, c, op, n):
            v, y, t, s = (nw[:, r, 0:n] for r in range(4))
            link(dve.tensor_scalar(v, src, c, None, op))
            link(dve.tensor_scalar(y.bitcast(I32), v.bitcast(I32), -0.5, float(0x5F3759DF), ALU.mult, ALU.add))
            for _ in range(3):
                link(dve.tensor_tensor(t, y, y, ALU.mult))
                link(dve.scalar_tensor_tensor(s, t, -0.5, v, ALU.mult, ALU.mult))
                link(dve.scalar_tensor_tensor(y, s, 1.5, y, ALU.add, ALU.mult))

        def token_moments(dve, link):
            for t in range(TILES):
                ins = dve.bn_stats(stat[:, t, :], xn_tok[:, t, :])
            link(ins)
            for t in range(TILES):
                ins = dve.bn_aggr(mv[:, t, :], stat[:, t, :])
            link(ins)
            inv_root(dve, link, mv[:, :, 1], EPS, ALU.add, TILES)

        def norm_tokens(dve, link):
            token_moments(dve, link)
            for t in range(TILES):
                ins = dve.tensor_scalar(xn_tok[:, t, :], xn_tok[:, t, :], mv[:, t, 0:1], nw[:, 1, t:t + 1],
                                        ALU.subtract, ALU.mult)
            link(ins)

        def keep_moments(dve, link):
            token_moments(dve, link)
            dve.tensor_copy(xn_stat[:, :, 0], mv[:, :, 0])
            link(dve.tensor_copy(xn_stat[:, :, 1], nw[:, 1, 0:TILES]))

        with nc.Block() as block:
            @block.sync
            def _(sp):
                sp.dma_start(xn_tok[:, :, :], tokens(x, 0)).then_inc(first_x, 16)
                for dst, src in ((wa_s[:, :], wa), (vec_s[:, :], vec), (wo_s[:, :, :], wo), (wf1_s[:, :], wf1),
                                 (wvr_s, wvr), (w1_s[:, :, :], w1)):
                    sp.dma_start(dst, src).then_inc(s_load, 16)
                sp.dma_start(tab_s[:, 4:6, :], tabs[:, 4:6, :]).then_inc(tab_a_in, 16)
                sp.dma_start(wb_s[:, :, :], wb).then_inc(late_in, 16)
                sp.dma_start(tab_s[:, 0:4, :], tabs[:, 0:4, :]).then_inc(tab_b_in, 16)

            @block.scalar
            def _(act):
                for dst, src in ((ident_s[:, :], ident), (center_s[:, :], center), (ones_s[:, :], ones), (sum_s[:, :, :], sum_heads),
                                 (pick_s[:, :], pick), (cbf_s[:, :], cbf)):
                    act.dma_start(dst, src).then_inc(s_load, 16)
                for dst, src in ((wf2_s[:, :, :], wf2), (wob_s[:, :, :, :], wob), (w2_s[:, :, :, :], w2)):
                    act.dma_start(dst, src).then_inc(late_in, 16)

            @block.gpsimd
            def _(pool):
                pool.memset(vB[:, :, :, B_HD:2 * B_HD], 1.0).then_inc(setup_p, 1)
                pool.memset(vA[:, :, :, A_HD:32], 1.0).then_inc(setup_p, 1)
                pool.memset(xT[:, 0:1], 0.0).then_inc(setup_p, 1)
                pool.memset(eps_s[:, :], EPS).then_inc(setup_p, 1)
                pool.memset(mT[:, :, :], 0.0).then_inc(setup_p, 1)

            @block.tensor
            def _(pe):
                pe.wait_ge(s_load, 16 * 12)
                for n, (w, b, _) in enumerate(biases):
                    pe.matmul(bank[0:w.shape[1], 0, n:n + 1], w, vec_s[:, b:b + 1], start=True, stop=True)
                pe.matmul(bank[:, 0, NB:NB + 1], wvr_s, vec_s[:, V_B1:V_B1 + 1],
                          start=True, stop=True).then_inc(setup_mm, 1)
                pe.wait_ge(setup_v, 1)
                for j in range(A_GRP):
                    mm = pe.matmul(bank[:, 1, 0:1], wo_s[:, j, :], bias[:, V_BVR:V_BVR + 1],
                                   start=(j == 0), stop=(j == A_GRP - 1))
                mm.then_inc(setup_mm, 1)

            @block.vector
            def _(dve):
                dve.wait_ge(first_x, 16)
                link = linker(dve, setup_link)
                norm_tokens(dve, link)
                keep_moments(dve, link)
                dve.wait_ge(s_load, 16 * 12)
                dve.wait_ge(setup_mm, 1)
                dve.tensor_tensor(bias[:, V_BVR:V_BVR + 1], bank[:, 0, NB:NB + 1], vec_s[:, V_BVR:V_BVR + 1],
                                  ALU.add).then_inc(setup_v, 1)
                for n, (w, _, dst) in enumerate(biases):
                    m = w.shape[1]
                    dve.tensor_tensor(bias[0:m, dst:dst + 1], bank[0:m, 0, n:n + 1], vec_s[0:m, dst:dst + 1],
                                      ALU.add).then_inc(setup_v, 1)
                dve.tensor_scalar(wa_s[:, :], wa_s[:, :], vec_s[:, V_G1:V_G1 + 1], None, ALU.mult).then_inc(setup_v, 1)
                dve.tensor_scalar(wf1_s[:, :], wf1_s[:, :], vec_s[:, V_G2:V_G2 + 1], None,
                                  ALU.mult).then_inc(setup_v, 1)
                for l in range(LAYERS):
                    g = V_L + l * VL_N + VL_G
                    dve.tensor_scalar(w1_s[:, l, :], w1_s[:, l, :], vec_s[:, g:g + 1], None,
                                      ALU.mult).then_inc(setup_v, 1)
                dve.wait_ge(setup_mm, 2)
                dve.tensor_tensor(bias[:, V_BO:V_BO + 1], bank[:, 1, 0:1], vec_s[:, V_BO:V_BO + 1],
                                  ALU.add).then_inc(setup_v, 1)

        KEPT = {1: pc[:, 0, :], 2: pc[:, 1, :], 4: ps_[:, 0, :], 5: ps_[:, 1, :], 7: norm_more[:, 0, :]}

        def pair(br, c, k):
            return c * 5 + k if br < 0 else 10 + br * 16 + c * 8 + k

        def taken(eng, i):
            eng.wait_ge(drained[i % RING], i // RING + 1)

        def use_wait(eng, i):
            if i >= RING:
                eng.wait_ge(drained[i % RING], i // RING)

        h_tok = oT[:, 0, :].rearrange("p (t d) -> p t d", d=D)

        def ln_n(name, c):
            return {"a_ln": 0, "ln0": 1, "ln1": 2}[name] * CHUNKS + c

        def values_use(br, t):
            return USE0["a_proj"] + 20 if br < 0 else USE0[f"v{br}{t // TPC}"] + t % TPC

        RAW0 = {0: 2, 1: 2 + 16 + 2}

        LAST_UNIT = {-1: A_UNITS - 1, 0: A_UNITS + B_UNITS - 1, 1: UNITS - 1}
        FIRST_UNIT = {-1: 0, 0: A_UNITS, 1: A_UNITS + B_UNITS}

        with nc.Fori(0, BATCH) as b:
            with nc.Block() as block:
                out_b = tokens(out, b)

                @block.sync
                def _(sp):
                    sp.dma_start(x_tok[:, :, :], tokens(x, b)).then_inc(x_in, 16)
                    sp.wait_ge(tok_norm, TILES)
                    sp.wait_ge(mm_full, 4)
                    sp.dma_start(xn_tok[:, :, :], tokens(x, b + 1)).then_inc(next_in, 16)
                    for jb in range(LAYERS * CHUNKS * B_QK):
                        l, slot = jb // (CHUNKS * B_QK), jb % 4
                        sp.wait_ge(raw_rdy, RAW0[l] + jb % (CHUNKS * B_QK) + 1)
                        if jb >= 4:
                            sp.wait_ge(prod_rdy, jb - 3)
                        for r in range(2):
                            sp.dma_start(rot[r::2, slot, :], raw[1 - r::2, slot, :]).then_inc(rot_rdy[slot], 16)
                    for c in range(CHUNKS):
                        sp.wait_ge(out_rdy, c + 1)
                        sp.dma_start(out_b[:, c * TPC:(c + 1) * TPC, :],
                                     x_tok[:, c * TPC:(c + 1) * TPC, :]).then_inc(out_done, 16)
                    sp.wait_ge(out_done, 16 * CHUNKS)

                @block.gpsimd
                def _(pool):
                    pool.memset(kA[:, :, :].bitcast(F32), 0.0).then_inc(kz_rdy, 1)
                    for br in (-1, 0, 1):
                        for c in range(CHUNKS):
                            for k in range(5 if br < 0 else B_QK):
                                j = pair(br, c, k)
                                if br < 0:
                                    taken(pool, USE0["a_proj"] + c * 10 + 2 * k)
                                    taken(pool, USE0["a_proj"] + c * 10 + 2 * k + 1)
                                    if j >= 2:
                                        pool.wait_ge(split_rdy, j - 1)
                                    dst = raw[:, j % 2, :]
                                else:
                                    pool.wait_ge(prod_rdy, j - 10 + 1)
                                    dst = qk[:, k, cc(c)]
                                if br >= 0 and c == 0 and k == 0:
                                    pool.wait_ge(st_full, FIRST_UNIT[br])
                                pool.tensor_tensor(dst, pc[:, j % 2, :], ps_[:, j % 2, :],
                                                   ALU.add).then_inc(sum_rdy, 1)

                @block.tensor
                def _(pe):
                    def product(i, parts, signal=True):
                        use_wait(pe, i)
                        m = parts[0][0].shape[1]
                        n = parts[0][1].shape[1]
                        for q, (lhs, rhs) in enumerate(parts):
                            mm = pe.matmul(bank[0:m, i % RING, 0:n], lhs, rhs, start=(q == 0),
                                           stop=(q == len(parts) - 1))
                        mm.then_inc(mm_full, 1)

                    def scores(n):
                        br, t, g = unit(n)
                        A = br < 0
                        w = P if t == 0 else P + (A_WIN if A else B_WIN)
                        if n - FIRST_UNIT[br] >= 2:
                            pe.wait_ge(max_rdy, n - 1)
                        elif n - FIRST_UNIT[br] == 0:
                            stop = USE0["a_norm"] if A else USE0[f"wo{br}"]
                            for i in range(stop - RING, stop):
                                taken(pe, i)
                        if A:
                            pe.wait_ge(split_rdy, pair(br, t // TPC, 4) + 1)
                            pe.wait_ge(ka_rdy, t // TPC + 1)
                        else:
                            pe.wait_ge(round_rdy, br * TILES + t + 1)
                        mask = (smask0 if t == 0 else smask)[min(br, 0)]
                        q0, k0 = t * P, (t + 1) * P - w
                        for h in range(4):
                            dst = s_bank[n % 2][:, h // 2, :]
                            if h % 2 == 0:
                                pe.matmul(dst[:, 0:2 * w], identb, mask, start=True, stop=False,
                                          skip_group_check=True)
                            if A:
                                mm = pe.matmul(dst[:, (h % 2) * w:(h % 2 + 1) * w], qA[:, h, q0:q0 + P],
                                               kA[:, g, k0:k0 + w], start=False, stop=(h % 2 == 1),
                                          skip_group_check=True)
                            else:
                                r = slice(64 * g, 64 * g + 64)
                                mm = pe.matmul(dst[:, (h % 2) * w:(h % 2 + 1) * w], qR[r, t % 2, h, :],
                                               kR[r, t % 2, h, 0:w], start=False, stop=(h % 2 == 1),
                                               skip_group_check=True)
                        mm.then_inc(sc_full, 1)

                    def turn_max(n):
                        pe.wait_ge(max_rdy, n + 1)
                        if n >= 1:
                            pe.wait_ge(mt_rdy, n)
                        pe.transpose(x_bank[0:8, 0:64].bitcast(BF16), negm[:, n % 2, :], identb).then_inc(mt_full, 1)

                    def key_scores(n):
                        br, t, g = unit(n)
                        A = br < 0
                        win = A_WIN if A else B_WIN
                        pe.wait_ge(mt_rdy, n + 1)
                        if n >= 1:
                            pe.wait_ge(exp_done, n)
                        q0 = t * P
                        rows = slice(64 * g, 64 * g + 64)
                        pe.matmul(t_bank, identb, tmask[min(br, 0)], start=True, stop=False, skip_group_check=True)
                        for h in range(4):
                            pe.matmul(t_bank[:, h * P:(h + 1) * P], selm[:, h * P:(h + 1) * P], mT[:, n % 2, :],
                                      start=False, stop=False, skip_group_check=True)
                        if t:
                            pe.matmul(c_bank[:, 0:4 * win], identb, cmask[min(br, 0)],
                                      start=True, stop=False, skip_group_check=True)
                            for h in range(4):
                                pe.matmul(c_bank[:, h * win:(h + 1) * win], selm[:, h * P:(h + 1) * P],
                                          mT[:, n % 2, 0:win], start=False, stop=False, skip_group_check=True)
                        if A:
                            if t:
                                pe.matmul(c_bank[:, 0:4 * win], kA[:, g, q0 - P:q0], qA[:, :, q0:q0 + win],
                                          start=False, stop=True, skip_group_check=True)
                            mm = pe.matmul(t_bank, kA[:, g, q0:q0 + P], qA[:, :, q0:q0 + P], start=False, stop=True,
                                           skip_group_check=True)
                        else:
                            if t:
                                for h in range(4):
                                    pe.matmul(c_bank[:, h * win:(h + 1) * win], qk[rows, 4 + h, q0 - P:q0],
                                              qk[rows, h, q0:q0 + win], start=False, stop=(h == 3),
                                              skip_group_check=True)
                            for h in range(4):
                                mm = pe.matmul(t_bank[:, h * P:(h + 1) * P], qk[rows, 4 + h, q0:q0 + P],
                                               qk[rows, h, q0:q0 + P], start=False, stop=(h == 3),
                                               skip_group_check=True)
                        mm.then_inc(st_full, 1)

                    def weigh(n):
                        br, t, g = unit(n)
                        pe.wait_ge(exp_done, n + 1)
                        taken(pe, values_use(br, t))
                        if br < 0:
                            if g == 0 and t:
                                pe.wait_ge(ot_rdy, t)
                            rows = slice(32 * g, 32 * g + 32)
                            mm = pe.matmul(o_bank[rows, :], vA[:, t, g, :], pm[:, n % 2, :], start=True, stop=(t == 0),
                                           skip_group_check=True)
                            if t:
                                dst = o_bank[rows, :].rearrange("p (h q) -> p h q", h=4)[:, :, 0:A_WIN]
                                mm = pe.matmul(dst, vA[:, t - 1, g, :], pcor[:, n % 2, 0:4 * A_WIN], start=False,
                                               stop=True, skip_group_check=True)
                        else:
                            if n == A_UNITS:
                                pe.wait_ge(ot_rdy, TILES)
                            else:
                                pe.wait_ge(ob_rdy, n - A_UNITS)
                            cols = slice(B_HD * g, B_HD * (g + 2))
                            for h in range(4):
                                mm = pe.matmul(o_bank[:, h * P:(h + 1) * P], vB[:, t, h, cols],
                                               pm[:, n % 2, h * P:(h + 1) * P], start=(h == 0), stop=(t == 0),
                                               skip_group_check=True)
                            for h in range(4 if t else 0):
                                mm = pe.matmul(o_bank[:, h * P:h * P + B_WIN], vB[:, t - 1, h, cols],
                                               pcor[:, n % 2, h * B_WIN:(h + 1) * B_WIN], start=False, stop=True,
                                               skip_group_check=True)
                        mm.then_inc(pv_done, 1)

                    def attention(br):
                        n0, n1 = FIRST_UNIT[br], LAST_UNIT[br]
                        scores(n0)
                        for n in range(n0, n1 + 1):
                            turn_max(n)
                            if n < n1:
                                scores(n + 1)
                            if n >= n0 + 2:
                                weigh(n - 2)
                            key_scores(n)
                        weigh(n1 - 1)
                        weigh(n1)

                    def layernorm(name, src, ready):
                        for c in range(CHUNKS):
                            ready(c)
                            product(USE0[name] + c, [(center_s[:, :], src(c))])

                    def ln_mean(name):
                        for c in range(CHUNKS):
                            taken(pe, USE0[name] + c)
                            product(USE0[f"{name}_mean"] + c,
                                    [(ones_s[:, 0:P], (oT[:, 1, cc(c)] if name == "a_ln" else sq[:, c, :]))])

                    def a_hidden(c, half):
                        pe.wait_ge(hn_rdy, c + 1)
                        for q in range(2):
                            f = 2 * half + q
                            product(USE0[f"a_hid{c}{half}"] + q, [(wf1_s[:, f * P:(f + 1) * P], hA[:, cc(c)])])

                    def a_output(c):
                        for half in range(2):
                            for q in range(2):
                                taken(pe, USE0[f"a_hid{c}{half}"] + q)
                        product(USE0[f"a_out{c}"], [(wf2_s[:, f, :], oT[:, f, cc(c)]) for f in range(4)])

                    for c in range(CHUNKS):
                        for w in range(2):
                            i = USE0["in"] + 2 * c + w
                            use_wait(pe, i)
                            if w:
                                pe.wait_ge(tok_norm, (c + 1) * TPC)
                            for tt in range(TPC):
                                t = c * TPC + tt
                                tok = (xn_tok if w == 0 else h_tok)[:, t, :]
                                mm = pe.transpose(bank[:, i % RING, tt * P:(tt + 1) * P], tok, ident_s[:, :])
                            mm.then_inc(mm_full, 1)
                    u = USE0["a_proj"]
                    for c in range(CHUNKS):
                        taken(pe, USE0["in"] + 2 * c + 1)
                        for k in range(5):
                            w0 = WA_Q + (k - 1) * P if k else WA_K
                            w1_ = WA_QR + (k - 1) * P if k else WA_KR
                            product(u + c * 10 + 2 * k, [(wa_s[:, w0:w0 + P], hT[:, cc(c)])])
                            product(u + c * 10 + 2 * k + 1, [(wa_s[:, w1_:w1_ + P], hT[:, cc(c)])])
                    use_wait(pe, u + 20)
                    for t in range(TILES):
                        mm = pe.matmul(bank[:, (u + 20) % RING, t * 32:(t + 1) * 32], hT[:, t * P:(t + 1) * P],
                                       wa_s[:, WA_V:WA_V + 32], start=True, stop=True)
                    mm.then_inc(mm_full, 1)
                    attention(-1)
                    for i in range(8):
                        pe.wait_ge(rec_rdy, (i // 4 + 1) * TPC * A_GRP)
                        product(USE0["a_norm"] + i, [(pick_s[:, :], rec[:, i % 4, cc(i // 4)])])
                    for c in range(CHUNKS):
                        for j in range(4):
                            taken(pe, USE0["a_norm"] + 4 * c + j)
                        product(USE0["a_wo"] + c, [(wo_s[:, j, :], oT[:, j, cc(c)]) for j in range(4)])
                    layernorm("a_ln", lambda c: aT[:, cc(c)], lambda c: taken(pe, USE0["a_wo"] + c))

                    pe.wait_ge(late_in, 16 * 4)
                    for l in range(LAYERS):
                        def sum_squares(c, k):
                            j = pair(l, c, k)
                            taken(pe, qk_use(l, c, k))
                            pe.matmul(bank[0:16, 4 + c, :], sum_s[:, k, :], sq[:, j % 2, :], start=(k == 0),
                                      stop=(k == B_QK - 1)).then_inc(ss_done, 1)

                        def turn_sums(c):
                            pe.wait_ge(sums_copied, l * CHUNKS + c + 1)
                            for tt in range(TPC):
                                mm = pe.transpose(bank[:, 4 + c, tt * 16:(tt + 1) * 16],
                                                  ss[0:16, c, tt * P:(tt + 1) * P], ident_s[0:16, 0:16])
                            mm.then_inc(sums_turned, 1)

                        def turn_norms(c):
                            pe.wait_ge(rsp_rdy, l * CHUNKS + c + 1)
                            for tt in range(TPC):
                                mm = pe.transpose(bank[0:48, 6 + c, tt * 64:(tt + 1) * 64].bitcast(BF16),
                                                  rsp[:, c, tt, :], identb)
                            mm.then_inc(rt_full, 1)

                        def spread_norms(c, tiles):
                            pe.wait_ge(rt_rdy, l * CHUNKS + c + 1)
                            for k in tiles:
                                product(norm_use(l, c, k), [(seln[:, k * P:(k + 1) * P], rT[:, c, :])])

                        for c in range(CHUNKS):
                            pe.wait_ge(shift_rdy, l * 4 + c + 1)
                            for k in range(B_QK):
                                u = qk_use(l, c, k)
                                product(u, [(wb_s[:, l, k * P:(k + 1) * P], hT[:, cc(c)])])
                                if k:
                                    sum_squares(c, k - 1)
                                if c and k == 3:
                                    turn_norms(0)
                                if c and k >= 4:
                                    spread_norms(0, (2 * k - 8, 2 * k - 7))
                            if l == 0 and c == 0:
                                ln_mean("a_ln")
                            for tt in range(TPC):
                                t = c * TPC + tt
                                product(USE0[f"v{l}{c}"] + tt, [(hT[:, t * P:(t + 1) * P], wb_s[:, l, 1024:1536])])
                                if tt == 0:
                                    sum_squares(c, B_QK - 1)
                                if tt == 1:
                                    turn_sums(c)
                        turn_norms(1)
                        spread_norms(1, range(B_QK))
                        attention(l)
                        for c in range(CHUNKS):
                            pe.wait_ge(on_rdy, (l * TILES + (c + 1) * TPC) * 2)
                            product(USE0[f"wo{l}"] + c, [(wob_s[:, l, f, :], oT[:, f, cc(c)]) for f in range(4)])
                        a_hidden(l, 0)
                        layernorm(f"ln{l}", lambda c: hT[:, cc(c)],
                                  lambda c: pe.wait_ge(shift_rdy, l * 4 + 2 + c + 1))
                        a_hidden(l, 1)
                        ln_mean(f"ln{l}")
                        a_output(l)

                        def mlp_hidden(c, tiles):
                            pe.wait_ge(hn_rdy, (l + 1) * CHUNKS + c + 1)
                            for f in tiles:
                                start, w = HID_T[f]
                                for part in range(2):
                                    at = part * HID + start
                                    product(ffn_use(l, c, 2 * f + part), [(w1_s[:, l, at:at + w], hT[:, cc(c)])])

                        def mlp_output(c):
                            for f in range(3):
                                taken(pe, ffn_use(l, c, 2 * f))
                            product(ffn_use(l, c, 6), [(w2_s[0:w, l, f, :], oT[0:w, f, cc(c)])
                                                       for f, (_, w) in enumerate(HID_T)])

                        mlp_hidden(0, (0, 1, 2))
                        mlp_hidden(1, (0,))
                        mlp_output(0)
                        mlp_hidden(1, (1, 2))
                        mlp_output(1)
                    for c in range(CHUNKS):
                        i = USE0["out"] + c
                        pe.wait_ge(fin_rdy, c + 1)
                        use_wait(pe, i)
                        for tt in range(TPC):
                            t = c * TPC + tt
                            mm = pe.transpose(bank[:, i % RING, tt * P:(tt + 1) * P], aT[:, t * P:(t + 1) * P],
                                              ident_s[:, :])
                        mm.then_inc(mm_full, 1)

                @block.scalar
                def _(act):
                    def attention(br):
                        A = br < 0
                        win = A_WIN if A else B_WIN
                        scale = A_HD ** -0.5 if A else 8.0

                        def copy_max(n):
                            act.wait_ge(mt_full, n + 1)
                            if n >= 2:
                                act.wait_ge(st_full, n - 1)
                            act.activation(mT[0:8, n % 2, :], x_bank[0:8, 0:64].bitcast(BF16), ACT.Copy)\
                               .then_inc(mt_rdy, 1)

                        def copy_heads(t):
                            act.wait_ge(pv_done, (t + 1) * A_KV)
                            o = o_bank.rearrange("p (f q) -> p f q", f=4)
                            act.activation(rec[:, :, t * P:(t + 1) * P], o, ACT.Identity,
                                           bias=vec_s[:, V_HEAD:V_HEAD + 1], scale=vec_s[:, V_SUM:V_SUM + 1])
                            act.activation(oT[:, :, t * P:(t + 1) * P], o, ACT.Copy).then_inc(ot_rdy, 1)

                        def copy_out(n):
                            _, t, g = unit(n)
                            own, other = slice(64 * g, 64 * g + 64), slice(64 * (1 - g), 64 * (1 - g) + 64)
                            act.wait_ge(pv_done, n + 1)
                            if br * TILES + t >= 2:
                                act.wait_ge(on_rdy, (br * TILES + t - 1) * 2)
                            act.activation(oT[own, :, t * P:(t + 1) * P],
                                           o_bank[own, :].rearrange("p (f q) -> p f q", f=4), ACT.Copy)
                            act.activation(sums[own, t % 2, :], o_bank[other, :], ACT.Copy).then_inc(ob_rdy, 1)

                        def round_tile(t):
                            w = P if t == 0 else P + B_WIN
                            if t < TPC:
                                for k in range(B_QK - RING, B_QK):
                                    taken(act, norm_use(br, 0, k))
                            else:
                                act.wait_ge(late_scaled, (br + 1) * len(KEPT))
                            if t == 0:
                                act.wait_ge(sum_rdy, pair(br, CHUNKS - 1, B_QK - 1) + 1)
                            elif t >= 2:
                                act.wait_ge(sc_full, FIRST_UNIT[br] + 2 * (t - 1))
                            act.activation(qR[:, t % 2, :, :], qk[:, 0:4, t * P:(t + 1) * P], ACT.Copy)
                            act.activation(kR[:, t % 2, :, 0:w], qk[:, 4:8, (t + 1) * P - w:(t + 1) * P],
                                           ACT.Copy).then_inc(round_rdy, 1)

                        if not A:
                            round_tile(0)
                            for k, buf in KEPT.items():
                                i = norm_use(br, 1, k)
                                act.wait_ge(mm_full, i + 1)
                                act.activation(buf, bank[:, i % RING, :], ACT.Copy).then_inc(drained[i % RING], 1)
                        for n in range(FIRST_UNIT[br], LAST_UNIT[br] + 1):
                            _, t, g = unit(n)
                            if not A and g == 0 and t + 1 < TILES:
                                round_tile(t + 1)
                            copy_max(n)
                            if not A and n >= FIRST_UNIT[br] + 2:
                                copy_out(n - 2)
                            if A and g == 1 and t:
                                copy_heads(t - 1)
                            act.wait_ge(st_full, n + 1)
                            if n >= 2:
                                act.wait_ge(pv_done, n - 1)
                            if t:
                                act.activation(pcor[:, n % 2, 0:4 * win], c_bank[:, 0:4 * win], ACT.Exp, scale=scale)
                            act.activation(pm[:, n % 2, :], t_bank, ACT.Exp, scale=scale).then_inc(exp_done, 1)
                        if A:
                            copy_heads(TILES - 1)
                        else:
                            copy_out(LAST_UNIT[br] - 1)
                            copy_out(LAST_UNIT[br])

                    def ln_buffers(name, c):
                        if name == "a_ln":
                            return [oT[:, r, cc(c)] for r in range(4)]
                        return [buf[:, c, :] for buf in (raw, sq, pc, ps_)]

                    def layernorm(name):
                        for c in range(CHUNKS):
                            i = USE0[name] + c
                            centred, square, _, _ = ln_buffers(name, c)
                            act.wait_ge(mm_full, i + 1)
                            act.activation(centred, bank[:, i % RING, :], ACT.Copy).then_inc(raw_rdy, 1)
                            act.activation(square, bank[:, i % RING, :], ACT.Square).then_inc(drained[i % RING], 1)

                    def ln_root(name):
                        u = USE0[f"{name}_mean"]
                        for c in range(CHUNKS):
                            act.wait_ge(mm_full, u + c + 1)
                            act.activation(ln_buffers(name, c)[2], bank[:, (u + c) % RING, :], ACT.Ln,
                                           bias=eps_s[:, 0:1]).then_inc(drained[(u + c) % RING], 1)
                        for c in range(CHUNKS):
                            taken(act, u + c)
                            _, _, log, root = ln_buffers(name, c)
                            act.activation(root, log, ACT.Exp, scale=-0.5).then_inc(rstd_rdy, 1)

                    def a_hidden(c, half):
                        for q in range(2):
                            i, f = USE0[f"a_hid{c}{half}"] + q, 2 * half + q
                            act.wait_ge(mm_full, i + 1)
                            act.activation(oT[:, f, cc(c)], bank[:, i % RING, :], ACT.Gelu,
                                           bias=bias[:, V_BF1 + f:V_BF1 + f + 1]).then_inc(drained[i % RING], 1)

                    for c in range(CHUNKS):
                        for w in range(2):
                            i = USE0["in"] + 2 * c + w
                            act.wait_ge(mm_full, i + 1)
                            act.activation(xc(c) if w == 0 else hT[:, cc(c)], bank[:, i % RING, :], ACT.Copy)\
                               .then_inc(drained[i % RING], 1)
                    for j in range(10):
                        if j == 9:
                            i = USE0["a_proj"] + 20
                            act.wait_ge(mm_full, i + 1)
                            act.activation(vA[:, :, :, 0:A_HD],
                                           bank[:, i % RING, 0:256].rearrange("p (t g d) -> p t g d", t=TILES, g=A_KV),
                                           ACT.Copy).then_inc(drained[i % RING], 1)
                        act.wait_ge(sum_rdy, j + 1)
                        if j >= 2:
                            act.wait_ge(split_rdy, j - 1)
                        act.activation(hiA[:, j % 2, :], raw[:, j % 2, :], ACT.Copy).then_inc(hi_rdy, 1)
                        if j % 5 == 1:
                            c = j // 5
                            act.wait_ge(split_rdy, j)
                            act.wait_ge(kz_rdy, 1)
                            for g in range(A_KV):
                                r = slice(32 * g, 32 * g + 32)
                                ins = act.activation(kA[r, g, cc(c)], kD[r, c, :].bitcast(F32), ACT.Copy)
                            ins.then_inc(ka_rdy, 1)
                    attention(-1)
                    layernorm("a_ln")
                    for l in range(LAYERS):
                        def copy_norms(c):
                            act.wait_ge(rt_full, l * CHUNKS + c + 1)
                            act.activation(rT[:, c, :], bank[0:48, 6 + c, 0:256].bitcast(BF16), ACT.Copy)\
                               .then_inc(rt_rdy, 1)

                        for c in range(CHUNKS):
                            for k in range(B_QK):
                                i, j = qk_use(l, c, k), pair(l, c, k)
                                jb = j - 10
                                act.wait_ge(mm_full, i + 1)
                                if jb >= 4:
                                    act.wait_ge(prod_rdy, jb - 3)
                                g = V_L + l * VL_N + VL_QS + k // 4
                                act.activation(raw[:, jb % 4, :], bank[:, i % RING, :], ACT.Identity,
                                               scale=vec_s[:, g:g + 1]).then_inc(raw_rdy, 1)
                                if jb >= 2:
                                    act.wait_ge(ss_done, jb - 1)
                                act.activation(sq[:, j % 2, :], bank[:, i % RING, :], ACT.Square)\
                                   .then_inc(drained[i % RING], 1)
                                if c and k == 3:
                                    copy_norms(0)
                            if l == 0 and c == 0:
                                ln_root("a_ln")
                            for tt in range(TPC):
                                i, t = USE0[f"v{l}{c}"] + tt, c * TPC + tt
                                if tt == 0:
                                    act.wait_ge(ss_done, (l * CHUNKS + c + 1) * B_QK)
                                    act.activation(ss[:, c, :], bank[0:16, 4 + c, :], ACT.Copy)\
                                       .then_inc(sums_copied, 1)
                                act.wait_ge(mm_full, i + 1)
                                act.wait_ge(pv_done, FIRST_UNIT[l])
                                v = bank[:, i % RING, :].rearrange("p (h g d) -> p h g d", h=4, g=2)
                                act.activation(vB[:, t, :, :].rearrange("p h (g d) -> p h g d", g=3)[:, :, 0::2, :],
                                               v, ACT.Copy).then_inc(drained[i % RING], 1)
                        copy_norms(1)
                        attention(l)
                        a_hidden(l, 0)
                        layernorm(f"ln{l}")
                        a_hidden(l, 1)
                        ln_root(f"ln{l}")
                        for c in range(CHUNKS):
                            for f, (s, w) in enumerate(HID_T):
                                i = ffn_use(l, c, 2 * f + 1)
                                n = (l * CHUNKS + c) * 3 + f
                                act.wait_ge(mm_full, i + 1)
                                before = c * 3 + f - 2
                                if before >= 0:
                                    taken(act, ffn_use(l, before // 3, 2 * (before % 3)))
                                bc = V_L + l * VL_N + VL_B1 + 3 + f
                                act.activation(gel[0:w, n % 2, :], bank[0:w, i % RING, :], ACT.Gelu,
                                               bias=bias[0:w, bc:bc + 1]).then_inc(drained[i % RING], 1)

                @block.vector
                def _(dve):
                    link = linker(dve, v_link)

                    def rotate(br, c, k, i, ct, st):
                        j = pair(br, c, k)
                        A = br < 0
                        if j >= 2:
                            dve.wait_ge(sum_rdy, j - 1)
                        if A:
                            bq, bqr = (V_BQ + k - 1, V_BQR + k - 1) if k else (V_BK, V_BKR)
                            dve.wait_ge(mm_full, i + 1)
                            dve.scalar_tensor_tensor(pc[:, j % 2, :], bank[:, i % RING, :], bias[:, bq:bq + 1], ct,
                                                     ALU.add, ALU.mult).then_inc(drained[i % RING], 1)
                            dve.wait_ge(mm_full, i + 2)
                            dve.scalar_tensor_tensor(ps_[:, j % 2, :], bank[:, (i + 1) % RING, :],
                                                     bias[:, bqr:bqr + 1], st, ALU.add, ALU.mult)\
                               .then_inc(drained[(i + 1) % RING], 1)
                        else:
                            jb = j - 10
                            dve.wait_ge(raw_rdy, RAW0[br] + c * 8 + k + 1)
                            dve.tensor_tensor(pc[:, j % 2, :], raw[:, jb % 4, :], ct, ALU.mult)
                            dve.wait_ge(rot_rdy[jb % 4], 32 * (jb // 4 + 1))
                            dve.tensor_tensor(ps_[:, j % 2, :], rot[:, jb % 4, :], st, ALU.mult).then_inc(prod_rdy, 1)

                    RAWLN = {"a_ln": 0, "ln0": 2 + 16, "ln1": 2 + 16 + 2 + 16}

                    def divide(i):
                        use, o = USE0["a_norm"] + i, oT[:, i % 4, cc(i // 4)]
                        dve.wait_ge(mm_full, use + 1)
                        dve.tensor_tensor(o, bank[:, use % RING, :], o, ALU.mult).then_inc(drained[use % RING], 1)

                    def attention(br):
                        A = br < 0
                        win = A_WIN if A else B_WIN

                        def maxima(n):
                            _, t, _ = unit(n)
                            w = P if t == 0 else P + win
                            dve.wait_ge(sc_full, n + 1)
                            if n >= 2:
                                dve.wait_ge(mt_full, n - 1)
                            link(dve.tensor_reduce(mx[:, n % 2, :],
                                                   s_bank[n % 2][:, :, 0:2 * w].rearrange("p b (h w) -> p b h w", h=2),
                                                   AX_X, ALU.max))
                            link(dve.tensor_scalar(negm[:, n % 2, 0:4], mx[:, n % 2, :], -1.0, None, ALU.mult))
                            dve.scalar_tensor_tensor(negm[:, n % 2, 4:8], mx[:, n % 2, :], -1.0, negm[:, n % 2, 0:4],
                                                     ALU.mult, ALU.subtract).then_inc(max_rdy, 1)

                        def invert(m):
                            t, h = divmod(m, A_GRP)
                            dve.wait_ge(ot_rdy, t + 1)
                            r = rec[:, h, t * P:(t + 1) * P]
                            dve.reciprocal(r, r).then_inc(rec_rdy, 1)

                        def scale_kept(m):
                            k = list(KEPT)[m]
                            i = norm_use(br, 1, k)
                            taken(dve, i)
                            dve.tensor_tensor(qk[:, k, cc(1)], KEPT[k], qk[:, k, cc(1)], ALU.mult)\
                               .then_inc(late_scaled, 1)

                        def normalise(m):
                            t, half = divmod(m, 2)
                            dve.wait_ge(ob_rdy, (br * TILES + t + 1) * 2)
                            q = slice(256 * half, 256 * (half + 1))
                            o = oT[:, 2 * half:2 * half + 2, t * P:(t + 1) * P]
                            link(dve.reciprocal(rl[:, half, :], sums[:, t % 2, q]))
                            dve.tensor_tensor(o, o, rl[:, half, :].rearrange("p (f q) -> p f q", f=2), ALU.mult)\
                               .then_inc(on_rdy, 1)

                        maxima(FIRST_UNIT[br])
                        if A:
                            split(CHUNKS - 1, A_GRP)
                        step, lag, count = (invert, A_GRP + 2, A_UNITS) if A else (normalise, 4, B_UNITS)
                        for n in range(FIRST_UNIT[br], LAST_UNIT[br] + 1):
                            m = n - FIRST_UNIT[br]
                            if n < LAST_UNIT[br]:
                                maxima(n + 1)
                            if m >= lag:
                                step(m - lag)
                            if not A and m < len(KEPT):
                                scale_kept(m)
                        for m in range(count - lag, count):
                            step(m)
                            if A and m >= count - 4:
                                divide(m - count + 4)

                    def layernorm(name):
                        for c in range(CHUNKS):
                            dve.wait_ge(raw_rdy, RAWLN[name] + c + 1)
                            dve.wait_ge(rstd_rdy, ln_n(name, c) + 1)
                            if name == "a_ln":
                                dst, centred, root = hA[:, cc(c)], oT[:, 0, cc(c)], oT[:, 3, cc(c)]
                            else:
                                dst, centred, root = hT[:, cc(c)], raw[:, c, :], ps_[:, c, :]
                            dve.tensor_tensor(dst, centred, root, ALU.mult).then_inc(hn_rdy, 1)

                    def shift(c):
                        dve.tensor_copy(hT[0:64, cc(c)], xT[0:64, 1 + c * CH:1 + (c + 1) * CH])
                        dve.tensor_copy(hT[64:128, cc(c)], xT[64:128, c * CH:(c + 1) * CH]).then_inc(shift_rdy, 1)

                    for t in range(TILES):
                        dve.tensor_scalar(h_tok[:, t, :], xn_tok[:, t, :], xn_stat[:, t, 0:1], xn_stat[:, t, 1:2],
                                          ALU.subtract, ALU.mult).then_inc(tok_norm, 1)
                    u = USE0["a_proj"]

                    def split(c, k):
                        j = pair(-1, c, k)
                        dve.wait_ge(hi_rdy, j + 1)
                        dst, sign = (qA[:, k - 1, cc(c)], V_SQ) if k else (kD[:, c, :], V_SK)
                        dve.scalar_tensor_tensor(dst, hiA[:, j % 2, :].bitcast(F32), vec_s[:, sign:sign + 1],
                                                 raw[:, j % 2, :], ALU.mult, ALU.add).then_inc(split_rdy, 1)

                    dve.wait_ge(tab_a_in, 16)
                    for j in range(10):
                        c, k = divmod(j, 5)
                        rotate(-1, c, k, u + c * 10 + 2 * k, tab_s[:, 4, cc(c)], tab_s[:, 5, cc(c)])
                        if j:
                            split(*divmod(j - 1, 5))
                    attention(-1)
                    for i in range(4, 8):
                        divide(i)
                    for c in range(CHUNKS):
                        shift(c)
                    for c in range(CHUNKS):
                        i = USE0["a_wo"] + c
                        dve.wait_ge(mm_full, i + 1)
                        dve.scalar_tensor_tensor(aT[:, cc(c)], bank[:, i % RING, :], bias[:, V_BO:V_BO + 1], xc(c),
                                                 ALU.add, ALU.add).then_inc(drained[i % RING], 1)
                    dve.wait_ge(tab_b_in, 16)
                    for l in range(LAYERS):
                        vl = V_L + l * VL_N
                        def norms(c):
                            dve.wait_ge(sums_turned, l * CHUNKS + c + 1)
                            inv_root(dve, link, bank[:, 4 + c, 0:64], 1e-24, ALU.max, 64)
                            y, r_ = nw[:, 1, :], nw[:, 2, :]
                            part = [rsp[:, c, :, 16 * m:16 * (m + 1)] for m in range(3)]
                            y, r_ = (z.rearrange("p (t k) -> p t k", t=TPC) for z in (y, r_))
                            link(dve.tensor_copy(part[0], y))
                            link(dve.tensor_tensor(r_, y, part[0], ALU.subtract))
                            link(dve.tensor_copy(part[1], r_))
                            dve.tensor_tensor(part[2], r_, part[1], ALU.subtract).then_inc(rsp_rdy, 1)

                        def scale(c, tiles):
                            for k in tiles:
                                i = norm_use(l, c, k)
                                dve.wait_ge(sum_rdy, pair(l, c, k) + 1)
                                dve.wait_ge(mm_full, i + 1)
                                dve.tensor_tensor(qk[:, k, cc(c)], bank[:, i % RING, :], qk[:, k, cc(c)], ALU.mult)\
                                   .then_inc(drained[i % RING], 1)

                        for c in range(CHUNKS):
                            for k in range(B_QK):
                                if c and k == 0:
                                    norms(0)
                                if c and k >= 4:
                                    scale(0, (2 * k - 8, 2 * k - 7))
                                r = 0 if k < 4 else 2
                                rotate(l, c, k, qk_use(l, c, k), tab_s[:, r, cc(c)], tab_s[:, r + 1, cc(c)])
                            if l == 0 and c == 0:
                                layernorm("a_ln")
                        norms(1)
                        scale(1, [k for k in range(B_QK) if k not in KEPT])
                        attention(l)
                        for c in range(CHUNKS):
                            i = USE0[f"wo{l}"] + c
                            dve.wait_ge(mm_full, i + 1)
                            dve.tensor_tensor(xc(c), bank[:, i % RING, :], xc(c), ALU.add)\
                               .then_inc(drained[i % RING], 1)
                            taken(dve, i)
                            shift(c)
                        if l == 0:
                            dve.wait_ge(next_in, 16)
                            norm_tokens(dve, link)
                        else:
                            keep_moments(dve, link)
                        i = USE0[f"a_out{l}"]
                        dve.wait_ge(mm_full, i + 1)
                        dve.scalar_tensor_tensor(aT[:, cc(l)], bank[:, i % RING, :], vec_s[:, V_BF2:V_BF2 + 1],
                                                 aT[:, cc(l)], ALU.add, ALU.add).then_inc(drained[i % RING], 1)
                        layernorm(f"ln{l}")

                        def gated(c, tiles):
                            for f in tiles:
                                w = HID_T[f][1]
                                i = ffn_use(l, c, 2 * f)
                                n = (l * CHUNKS + c) * 3 + f
                                dve.wait_ge(mm_full, i + 1)
                                taken(dve, i + 1)
                                bc = vl + VL_B1 + f
                                dve.scalar_tensor_tensor(oT[0:w, f, cc(c)], bank[0:w, i % RING, :],
                                                         bias[0:w, bc:bc + 1], gel[0:w, n % 2, :], ALU.add,
                                                         ALU.mult).then_inc(drained[i % RING], 1)

                        def mlp_sum(c):
                            i = ffn_use(l, c, 6)
                            dve.wait_ge(mm_full, i + 1)
                            dve.scalar_tensor_tensor(xc(c), bank[:, i % RING, :],
                                                     vec_s[:, vl + VL_B2:vl + VL_B2 + 1], xc(c), ALU.add,
                                                     ALU.add).then_inc(drained[i % RING], 1)
                            taken(dve, i)
                            if l + 1 < LAYERS:
                                shift(c)
                            else:
                                dve.tensor_tensor(aT[:, cc(c)], aT[:, cc(c)], xc(c), ALU.add).then_inc(fin_rdy, 1)

                        gated(0, (0, 1, 2))
                        gated(1, (0,))
                        mlp_sum(0)
                        gated(1, (1, 2))
                        mlp_sum(1)
                    dve.wait_ge(x_in, 16)
                    for c in range(CHUNKS):
                        i = USE0["out"] + c
                        dve.wait_ge(mm_full, i + 1)
                        tt = slice(c * TPC, (c + 1) * TPC)
                        dve.tensor_tensor(x_tok[:, tt, :], bank[:, i % RING, :].rearrange("p (t d) -> p t d", d=D),
                                          x_tok[:, tt, :], ALU.add).then_inc(out_rdy, 1)

            nc.all_engine_barrier(sems_to_clear=range(first, last + 1))



def pairwise():
    import numpy as np
    return np.arange(B_HD).reshape(2, B_HD // 2).T.ravel()


def host_constants():
    import numpy as np
    f = np.float32
    pos = np.arange(T, dtype=f)
    half = np.arange(0, B_HD, 2, dtype=f)
    inv = (f(1.0) / np.power(f(10000.0), half / f(B_HD))).astype(f)
    fr = (pos[:, None] * inv[None, :]).astype(f)
    fr = np.concatenate([fr, fr], axis=-1)
    base = ((half + f(0.4 * B_HD)) / f(1.4 * B_HD)).astype(f)
    power = ((pos - f(T // 2)) / f(B_WIN // 2)).astype(f)
    sc = np.power(base[None, :], power[:, None]).astype(f)
    sc = np.concatenate([sc, sc], axis=-1)
    sign = np.where(np.arange(B_HD) < B_HD // 2, f(-1), f(1))
    cos, sin = np.cos(fr).astype(f), np.sin(fr).astype(f) * sign
    cos, sin, sc = (z[:, pairwise()] for z in (cos, sin, sc))
    tabs = np.zeros((P, 6, T), f)
    for r, tab in enumerate((cos * sc, sin * sc, cos / sc, sin / sc)):
        tabs[:, r, :] = np.concatenate([tab, tab], axis=1).T
    th = (f(1.0) / np.power(f(10000.0), np.arange(A_HD // 2, dtype=f) / f(A_HD // 2))).astype(f)
    fr = (pos[:, None] * th[None, :]).astype(f)
    for row in range(P):
        d = row % A_HD
        a = fr[:, d % (A_HD // 2)]
        tabs[row, 4] = np.cos(a)
        tabs[row, 5] = np.sin(a) * (f(-1) if d < A_HD // 2 else f(1))
    ident = np.eye(P, dtype=f)
    center = (ident - f(1.0 / P)).astype(f)
    ones = np.full((P, P), 1.0 / P, f)
    sum_heads = np.zeros((P, B_QK, 16), f)
    for k in range(B_QK):
        sum_heads[:64, k, 2 * k] = 1
        sum_heads[64:, k, 2 * k + 1] = 1
    pick = np.zeros((P, P), f)
    for g in range(A_KV):
        pick[32 * g + A_HD, 32 * g:32 * g + 32] = 1
    r = np.arange(P)

    def allow(diff, win, strict):
        ok = (diff >= 0) & ((diff < win) if strict else (diff <= win))
        return np.where(ok, f(0), f(-1e30))

    parts = [ident]
    for win, s in ((A_WIN, True), (B_WIN, False)):
        parts.append(np.tile(allow(r[:, None] - (np.arange(P + win)[None, :] - win), win, s), (1, 2)))
    for win, s in ((A_WIN, True), (B_WIN, False)):
        parts.append(np.tile(allow(r[:, None] - r[None, :], win, s), (1, 2)))
    for win, s in ((A_WIN, True), (B_WIN, False)):
        parts.append(np.tile(allow(r[None, :] - r[:, None], win, s), (1, 4)))
    for win, s in ((A_WIN, True), (B_WIN, False)):
        parts.append(np.tile(allow(P + np.arange(win)[None, :] - r[:, None], win, s), (1, 4)))
    selm = np.zeros((P, 4, P), f)
    for h in range(4):
        selm[h, h] = 1
        selm[4 + h, h] = 1
    seln = np.zeros((P, B_QK, P), f)
    for k in range(B_QK):
        for m in range(3):
            seln[16 * m + 2 * k, k, :64] = 1
            seln[16 * m + 2 * k + 1, k, 64:] = 1
    parts += [selm.reshape(P, -1), seln.reshape(P, -1)]
    cbf = np.concatenate(parts, axis=1).astype(np.dtype("bfloat16"))
    return dict(tabs=tabs, ident=ident, center=center, ones=ones, sum_heads=sum_heads, pick=pick, cbf=cbf)


def host_layout(i):
    import numpy as np
    f = np.float32
    n = {k[3:]: np.asarray(v) for k, v in i.items()}
    wq, wk, wv = n["attn_Wq"], n["attn_Wk"], n["attn_Wv"]
    bq, bk, bv = n["attn_bq"], n["attn_bk"], n["attn_bv"]
    wa = np.zeros((P, WA_N), f)
    vec = np.zeros((P, V_N), f)
    wo = np.zeros((P, A_GRP, D), f)
    wvr = np.zeros((P, P), f)
    turn = (np.arange(A_HD) + A_HD // 2) % A_HD
    for g in range(A_KV):
        dup = [(32 * g + A_HD * m) for m in range(4)]
        for j in range(A_GRP):
            h = A_GRP * g + j
            for off, voff, cl in ((WA_Q, V_BQ, A_HD * h + np.arange(A_HD)), (WA_QR, V_BQR, A_HD * h + turn)):
                for r in dup:
                    wa[:, off + j * P + r:off + j * P + r + A_HD] = wq[:, cl]
                    vec[r:r + A_HD, voff + j] = bq[cl]
            wo[32 * g:32 * g + A_HD, j] = n["attn_Wo"][A_HD * h:A_HD * (h + 1)]
        for off, voff, cl in ((WA_K, V_BK, A_HD * g + np.arange(A_HD)), (WA_KR, V_BKR, A_HD * g + turn)):
            for r in dup:
                wa[:, off + r:off + r + A_HD] = wk[:, cl]
                vec[r:r + A_HD, voff] = bk[cl]
        wvr[:, 32 * g:32 * g + A_HD] = wv[:, A_HD * g:A_HD * (g + 1)]
        vec[32 * g:32 * g + A_HD, V_BVR] = bv[A_HD * g:A_HD * (g + 1)]
    wa[:, WA_V:] = wv
    blk = np.arange(P) % 32 // A_HD
    vec[:, V_SQ] = np.where(blk >= 2, f(-1), f(0))
    vec[:, V_SK] = np.where(blk % 2 == 1, f(-1), f(0))
    vec[:, V_SUM], vec[:, V_HEAD] = blk > 0, blk == 0
    for c, k in ((V_G1, "attn_g1"), (V_B1, "attn_b1"), (V_G2, "attn_g2"), (V_B2, "attn_b2"), (V_BO, "attn_bo"),
                 (V_BF2, "attn_bf2")):
        vec[:, c] = n[k]
    vec[:, V_BF1:V_BF1 + 4] = n["attn_bf1"].reshape(4, P).T
    wf2 = np.ascontiguousarray(n["attn_Wf2"].reshape(4, P, D).transpose(1, 0, 2))
    wqkv = n["ffn_wqkv"]
    order = np.concatenate([B_HD * h + pairwise() for h in range(2 * B_H)])
    wb = np.ascontiguousarray(np.concatenate([wqkv[:, :, order], wqkv[:, :, 1024:]], axis=2).transpose(1, 0, 2))
    wob = np.ascontiguousarray(n["ffn_wo"].reshape(LAYERS, 4, P, D).transpose(2, 0, 1, 3))
    w1 = np.ascontiguousarray(n["ffn_w1"].transpose(1, 0, 2))
    w2 = np.zeros((P, LAYERS, 3, P), f)
    for l in range(LAYERS):
        o = V_L + l * VL_N
        vec[:, o + VL_G], vec[:, o + VL_B], vec[:, o + VL_B2] = n["ffn_ln_g"][l], n["ffn_ln_b"][l], n["ffn_b2"][l]
        for q, k in enumerate("qk"):
            vec[:, o + VL_QS + q] = np.concatenate([n[f"ffn_{k}_scale"][l][pairwise()]] * 2)
        for hf in range(2):
            for t, (s, w) in enumerate(HID_T):
                vec[:w, o + VL_B1 + 3 * hf + t] = n["ffn_b1"][l, hf * HID + s:hf * HID + s + w]
        for t, (s, w) in enumerate(HID_T):
            w2[:w, l, t] = n["ffn_w2"][l, s:s + w]
    x = np.concatenate([n["attn_x"], n["attn_x"][:1]])
    return dict(x=x, wa=wa, wo=wo, wf1=n["attn_Wf1"], wf2=wf2, wvr=wvr, vec=vec, wb=wb,
                wob=wob, w1=w1, w2=w2)


def kernel(**inputs):
    import numpy as np
    import concourse.bacc as bacc
    from concourse.bass_utils import run_bass_kernel_spmd

    nc = bacc.Bacc("TRN2", target_bir_lowering=False, num_devices=1)
    arrays = {k: np.ascontiguousarray(v) for k, v in {**host_layout(inputs), **host_constants()}.items()}
    args = {k: nc.dram_tensor(k, v.shape, mybir.dt.from_np(v.dtype), kind="ExternalInput").ap()
            for k, v in arrays.items()}
    out = nc.dram_tensor("out", (BATCH, T, D), F32, kind="ExternalOutput").ap()
    program(nc, out=out, **args)
    return run_bass_kernel_spmd(nc, [arrays], core_ids=[0]).results[0]["out"]
```
